# Optimizing a Trainium2 kernel written in Bass

```python
import numpy as np
import jax
import jax.numpy as jnp

def _softmax(x, axis=-1):
    return jax.nn.softmax(x, axis=axis)

def _gelu(x):
    return jax.nn.gelu(x, approximate=True)

def _silu(x):
    return jax.nn.silu(x)

def _sigmoid(x):
    return jax.nn.sigmoid(x)

def _layernorm(x, axis=-1, eps=1e-05):
    m = jnp.mean(x, axis=axis, keepdims=True)
    v = jnp.var(x, axis=axis, keepdims=True)
    return (x - m) / jnp.sqrt(v + eps)

def _scatter_add(tgt, idx, src, axis=0):
    return tgt.at[idx].add(src)

def _segment_sum(src, seg, n):
    return jax.ops.segment_sum(src, seg, n)
kernel_name = 'mk_decoder_postln_d1_seqx_r4_0a3cdf'

def setup_inputs(seed: int=0):
    np.random.seed(seed)
    _w = jnp.asarray

    def _rec_inputs():
        import jax
        import jax.numpy as jnp
        _rk = jax.random.key(seed)
        x = 7.22e-05 + 1 * jax.random.normal(jax.random.fold_in(_rk, 1), (32, 128, 512), jnp.float32)
        _lenS = 128 - jax.random.randint(jax.random.fold_in(_rk, 7), (32,), 0, max(1, 128 // 4) + 1, jnp.int32)
        _lenS2 = 128 - jax.random.randint(jax.random.fold_in(_rk, 8), (32,), 0, max(1, 128 // 4) + 1, jnp.int32)
        _ctx_2048P = jax.random.normal(jax.random.fold_in(_rk, 11), (32, 16, 512), jnp.float32)
        _ctx_2048c = jax.random.dirichlet(jax.random.fold_in(_rk, 511), 0.3 * jnp.ones((16,), jnp.float32), (32, 128))
        _ctx_2048t = jnp.einsum('bsk,bkd->bsd', _ctx_2048c, _ctx_2048P)
        _ctx_2048t = _ctx_2048t * jax.lax.rsqrt(jnp.mean(jnp.square(_ctx_2048t)) + 1e-12) * 0.953939
        ctx_2048 = 4.13588e-05 + 0.999923 * (_ctx_2048t + 0.3 * jax.random.normal(jax.random.fold_in(_rk, 611), (32, 128, 512), jnp.float32))
        _validS = jnp.arange(128)[None, :] < _lenS[:, None]
        _validS2 = jnp.arange(128)[None, :] < _lenS2[:, None]
        _causal = jnp.tril(jnp.ones((128, 128), dtype=bool))
        mask_BxS2_bf1 = jnp.ones((32, 128), dtype=bool)
        return (x, ctx_2048, mask_BxS2_bf1)
    x, ctx_2048, mask_BxS2_bf1 = _rec_inputs()

    def _L0_attn_setup():
        import jax, jax.numpy as jnp
        import numpy as np
        DIM = 512
        STATE = 64
        DT_RANK = 128
        CHUNK = 128
        key = jax.random.key(seed)
        ks = jax.random.split(key, 8)
        B, L, D, N, R = (4, 512, DIM, STATE, DT_RANK)
        x = jax.random.normal(ks[0], (B, L, D), dtype=jnp.float32)
        norm_w = jnp.ones((D,), jnp.float32)
        norm_b = jnp.zeros((D,), jnp.float32)
        x_proj_w = jax.random.normal(ks[1], (R + 2 * N, D), jnp.float32) * (1.0 / np.sqrt(D))
        dt_proj_w = jax.random.normal(ks[2], (D, R), jnp.float32) * (1.0 / np.sqrt(R))
        dt_proj_b = jax.random.normal(ks[3], (D,), jnp.float32) * 0.01
        A_log = jnp.log(jnp.tile(jnp.arange(1, N + 1, dtype=jnp.float32)[None, :], (D, 1)))
        D_param = jnp.ones((D,), jnp.float32)
        out_proj_w = jax.random.normal(ks[4], (D, D), jnp.float32) * (1.0 / np.sqrt(D))
        return {'x': x, 'norm_w': norm_w, 'norm_b': norm_b, 'x_proj_w': x_proj_w, 'dt_proj_w': dt_proj_w, 'dt_proj_b': dt_proj_b, 'A_log': A_log, 'D_param': D_param, 'out_proj_w': out_proj_w}
    _L0_attn_all = _L0_attn_setup()
    _L0_attn_in = {k: v for k, v in _L0_attn_all.items() if k in ('norm_w', 'norm_b', 'x_proj_w', 'dt_proj_w', 'dt_proj_b', 'A_log', 'D_param', 'out_proj_w')}
    del _L0_attn_all

    def _L0_xattn_setup():
        import jax, jax.numpy as jnp
        import numpy as np
        import math
        D_MODEL = 512
        N_Q_HEADS = 16
        N_KV_HEADS = 4
        HEAD_DIM = D_MODEL // N_Q_HEADS
        B = 4
        S = 256

        def _alibi_slopes(num_heads):
            n = 2 ** int(math.floor(math.log2(num_heads)))
            m0 = 2.0 ** (-8.0 / n)
            return m0 ** jnp.arange(1, n + 1, dtype=jnp.float32)
        key = jax.random.key(seed)
        ks = jax.random.split(key, 8)
        xavier = lambda k, fi, fo: jax.random.normal(k, (fi, fo), jnp.float32) * math.sqrt(2.0 / (fi + fo))
        return {'query': jax.random.normal(ks[0], (B, S, D_MODEL), jnp.float32), 'key': jax.random.normal(ks[1], (B, S, D_MODEL), jnp.float32), 'value': jax.random.normal(ks[2], (B, S, D_MODEL), jnp.float32), 'mask': jnp.ones((B, S), dtype=bool), 'Wq': xavier(ks[3], D_MODEL, N_Q_HEADS * HEAD_DIM), 'Wk': xavier(ks[4], D_MODEL, N_KV_HEADS * HEAD_DIM), 'Wv': xavier(ks[5], D_MODEL, N_KV_HEADS * HEAD_DIM), 'Wo': xavier(ks[6], D_MODEL, D_MODEL)}
    _L0_xattn_all = _L0_xattn_setup()
    _L0_xattn_in = {k: v for k, v in _L0_xattn_all.items() if k in ('Wq', 'Wk', 'Wv', 'Wo')}
    del _L0_xattn_all

    def _L0_ffn_setup():
        import jax, jax.numpy as jnp
        import numpy as np
        B, S, D, I, E, K = (4, 256, 512, 256, 8, 2)
        key = jax.random.key(seed)
        ks = jax.random.split(key, 7)

        def w(k, shape, fan_in):
            return jax.random.normal(k, shape, dtype=jnp.float32) * fan_in ** (-0.5)
        return {'hidden_states': jax.random.normal(ks[0], (B, S, D), dtype=jnp.float32), 'router_w': w(ks[1], (D, E), D), 'gate_up_w': w(ks[2], (E, D, 2 * I), D), 'down_w': w(ks[3], (E, I, D), I), 'shared_gate_w': w(ks[4], (D, I), D), 'shared_up_w': w(ks[5], (D, I), D), 'shared_down_w': w(ks[6], (I, D), I)}
    _L0_ffn_all = _L0_ffn_setup()
    _L0_ffn_in = {k: v for k, v in _L0_ffn_all.items() if k in ('router_w', 'gate_up_w', 'down_w', 'shared_gate_w', 'shared_up_w', 'shared_down_w')}
    del _L0_ffn_all
    return {'x': x, 'ctx_2048': ctx_2048, 'mask_BxS2_bf1': mask_BxS2_bf1, 'L0_attn_norm_w': _L0_attn_in['norm_w'], 'L0_attn_norm_b': _L0_attn_in['norm_b'], 'L0_attn_x_proj_w': _L0_attn_in['x_proj_w'], 'L0_attn_dt_proj_w': _L0_attn_in['dt_proj_w'], 'L0_attn_dt_proj_b': _L0_attn_in['dt_proj_b'], 'L0_attn_A_log': _L0_attn_in['A_log'], 'L0_attn_D_param': _L0_attn_in['D_param'], 'L0_attn_out_proj_w': _L0_attn_in['out_proj_w'], 'L0_xattn_Wq': _L0_xattn_in['Wq'], 'L0_xattn_Wk': _L0_xattn_in['Wk'], 'L0_xattn_Wv': _L0_xattn_in['Wv'], 'L0_xattn_Wo': _L0_xattn_in['Wo'], 'L0_ffn_router_w': _L0_ffn_in['router_w'], 'L0_ffn_gate_up_w': _L0_ffn_in['gate_up_w'], 'L0_ffn_down_w': _L0_ffn_in['down_w'], 'L0_ffn_shared_gate_w': _L0_ffn_in['shared_gate_w'], 'L0_ffn_shared_up_w': _L0_ffn_in['shared_up_w'], 'L0_ffn_shared_down_w': _L0_ffn_in['shared_down_w']}

def reference(x, ctx_2048, mask_BxS2_bf1, L0_attn_norm_w, L0_attn_norm_b, L0_attn_x_proj_w, L0_attn_dt_proj_w, L0_attn_dt_proj_b, L0_attn_A_log, L0_attn_D_param, L0_attn_out_proj_w, L0_xattn_Wq, L0_xattn_Wk, L0_xattn_Wv, L0_xattn_Wo, L0_ffn_router_w, L0_ffn_gate_up_w, L0_ffn_down_w, L0_ffn_shared_gate_w, L0_ffn_shared_up_w, L0_ffn_shared_down_w):
    import jax
    import jax.numpy as jnp

    def _L0_attn_ref(x, norm_w, norm_b, x_proj_w, dt_proj_w, dt_proj_b, A_log, D_param, out_proj_w):
        import jax, jax.numpy as jnp
        import numpy as np
        DIM = 512
        STATE = 64
        DT_RANK = 128
        CHUNK = 128
        B, L, D = x.shape
        N = STATE
        mu = jnp.mean(x, axis=-1, keepdims=True)
        var = jnp.var(x, axis=-1, keepdims=True)
        xn = (x - mu) / jnp.sqrt(var + 1e-05) * norm_w + norm_b
        proj = xn @ x_proj_w.T
        R = dt_proj_w.shape[1]
        delta, B_ssm, C_ssm = jnp.split(proj, [R, R + N], axis=-1)
        delta = jax.nn.softplus(delta @ dt_proj_w.T + dt_proj_b)
        A = -jnp.exp(A_log)
        c_idx = jnp.arange(L) % CHUNK
        C_used = C_ssm[:, c_idx, :]

        def step(h, inp):
            dt, b, xt, c = inp
            dA = jnp.exp(dt[:, :, None] * A)
            h = dA * h + dt[:, :, None] * b[:, None, :] * xt[:, :, None]
            y = jnp.einsum('bdn,bn->bd', h, c)
            return (h, y)
        h0 = jnp.zeros((B, D, N), x.dtype)
        xs = (jnp.moveaxis(delta, 1, 0), jnp.moveaxis(B_ssm, 1, 0), jnp.moveaxis(xn, 1, 0), jnp.moveaxis(C_used, 1, 0))
        _, ys = jax.lax.scan(step, h0, xs)
        y = jnp.moveaxis(ys, 0, 1)
        return (y + x * D_param) @ out_proj_w.T

    def _L0_xattn_ref(query, key, value, mask, Wq, Wk, Wv, Wo):
        import jax, jax.numpy as jnp
        import numpy as np
        import math
        D_MODEL = 512
        N_Q_HEADS = 16
        N_KV_HEADS = 4
        HEAD_DIM = D_MODEL // N_Q_HEADS
        B = 4
        S = 256

        def _alibi_slopes(num_heads):
            n = 2 ** int(math.floor(math.log2(num_heads)))
            m0 = 2.0 ** (-8.0 / n)
            return m0 ** jnp.arange(1, n + 1, dtype=jnp.float32)
        b, q_len, d = query.shape
        kv_len = key.shape[1]
        G = N_KV_HEADS
        Hpg = N_Q_HEADS // G
        dh = HEAD_DIM
        Q = (query @ Wq).reshape(b, q_len, G, Hpg, dh)
        K = (key @ Wk).reshape(b, kv_len, G, dh)
        V = (value @ Wv).reshape(b, kv_len, G, dh)
        Q = Q / math.sqrt(dh)
        scores = jnp.einsum('bqghd,bkgd->bghqk', Q, K)
        rel = jnp.arange(kv_len, dtype=jnp.float32)[None, :] - jnp.arange(q_len, dtype=jnp.float32)[:, None]
        m = _alibi_slopes(N_Q_HEADS).reshape(1, G, Hpg, 1, 1)
        scores = scores + m * rel[None, None, None]
        neg = jnp.finfo(scores.dtype).min
        scores = jnp.where(mask[:, None, None, None, :], scores, neg)
        w = jax.nn.softmax(scores, axis=-1)
        out = jnp.einsum('bghqk,bkgd->bqghd', w, V)
        out = out.reshape(b, q_len, G * Hpg * dh)
        return out @ Wo

    def _L0_ffn_ref(hidden_states, router_w, gate_up_w, down_w, shared_gate_w, shared_up_w, shared_down_w):
        import jax, jax.numpy as jnp
        import numpy as np
        B, S, D, I, E, K = (4, 256, 512, 256, 8, 2)
        Bb, Ss, Dd = hidden_states.shape
        x = hidden_states.reshape(-1, Dd)
        T = x.shape[0]
        shared = jax.nn.silu(x @ shared_gate_w) * (x @ shared_up_w) @ shared_down_w
        logits = x @ router_w
        top_val, top_idx = jax.lax.top_k(logits, K)
        probs = jnp.zeros_like(logits).at[jnp.arange(T)[:, None], top_idx].set(jax.nn.sigmoid(top_val))
        xin = probs.T[:, :, None] * x[None]
        gu = jnp.einsum('etd,edf->etf', xin, gate_up_w)
        gate, up = jnp.split(gu, 2, axis=-1)
        h = jax.nn.silu(gate) * up
        expert_out = jnp.einsum('eti,eid->etd', h, down_w)
        combined = shared + expert_out.sum(axis=0)
        return combined.reshape(Bb, Ss, Dd)
    x = _layernorm(x + _L0_attn_ref(x, L0_attn_norm_w, L0_attn_norm_b, L0_attn_x_proj_w, L0_attn_dt_proj_w, L0_attn_dt_proj_b, L0_attn_A_log, L0_attn_D_param, L0_attn_out_proj_w), axis=-1)
    x = _layernorm(x + _L0_xattn_ref(x, ctx_2048, ctx_2048, mask_BxS2_bf1, L0_xattn_Wq, L0_xattn_Wk, L0_xattn_Wv, L0_xattn_Wo), axis=-1)
    x = _layernorm(x + _L0_ffn_ref(x, L0_ffn_router_w, L0_ffn_gate_up_w, L0_ffn_down_w, L0_ffn_shared_gate_w, L0_ffn_shared_up_w, L0_ffn_shared_down_w), axis=-1)
    return x

_drawn_inputs = setup_inputs


def setup_inputs(seed=0):
    import zlib

    import numpy as np

    out = dict(_drawn_inputs(seed))
    spreads = {'L0_attn_norm_w': (1.0, 0.2), 'L0_attn_norm_b': (0.0, 0.1), 'L0_attn_D_param': (1.0, 0.2)}
    factors = {'L0_attn_dt_proj_b': 2.906}
    for name, (base, spread) in spreads.items():
        noise = np.random.default_rng([zlib.crc32(name.encode()), seed]).standard_normal(out[name].shape)
        drawn = base * np.exp(spread * noise) if base else spread * noise
        out[name] = jnp.asarray(drawn.astype(out[name].dtype))
    for name, factor in factors.items():
        out[name] = (out[name] * factor).astype(out[name].dtype)
    return out
```

```python
from contextlib import ExitStack

import numpy as np

import concourse.bass as bass
from concourse import mybir

ALU = mybir.AluOpType
ACT = mybir.ActivationFunctionType
AX = mybir.AxisListType
F32 = mybir.dt.float32
BF16 = mybir.dt.bfloat16
U8 = mybir.dt.uint8

P = 128
B = 32
GB = 4
TG = GB * P
GROUPS = B // GB
D = 512
DC = D // P
NS = 64
NJ = 8
E = 8
NI = 256
NE = E + 1
HEADS = 16
KV = 4
HPG = HEADS // KV
DH = D // HEADS
EPS = 1e-5
NEG = float(np.finfo(np.float32).min)

DVE_LINKS = 55
ACT_LINKS = 8
LN_PASS = 4


def decoder_layer_kernel(nc, a, out):
    ctx = ExitStack()
    with ctx:
        def sb(name, shape, dt=F32):
            return ctx.enter_context(nc.sbuf_tensor(name, shape, dt))

        def sem(name):
            return ctx.enter_context(nc.semaphore(name))

        w_xproj = sb("w_xproj", [P, DC, P + 4 * NS])
        w_dt = sb("w_dt", [P, D])
        w_out = sb("w_out", [P, DC, D])
        w_q = sb("w_q", [P, DC, D])
        w_k = sb("w_k", [P, DC, P])
        w_v = sb("w_v", [P, DC, P])
        w_o = sb("w_o", [P, DC, D])
        w_router = sb("w_router", [P, DC, E])
        chan = sb("chan", [P, 4, DC])
        a_neg = sb("a_neg", [P, DC, NS])
        d_diag = sb("d_diag", [P, DC, P])
        ident = sb("ident", [P, P])
        identb = sb("identb", [P, P], BF16)
        pick_hm = sb("pick_hm", [P, NS + 1], BF16)
        pick_lob = sb("pick_lob", [P, NS + 1], BF16)
        pick_loc = sb("pick_loc", [P, NS + 1], BF16)
        pick_p = sb("pick_p", [25, NE], BF16)
        picks32 = sb("picks32", [P, 3, NS + 1])
        pickp32 = sb("pickp32", [25, NE])
        alibi = sb("alibi", [P, HPG, KV, P])
        tri = sb("tri", [P, E, E])
        masks = sb("masks", [P, B, P], U8)

        x_raw = sb("x_raw", [P, GB, D])
        x1 = sb("x1", [P, GB, D])
        ctx_raw = sb("ctx_raw", [P, GB, D])
        acc = sb("acc", [P, GB, D])
        x2T = sb("x2T", [P, DC, TG])
        xnT = sb("xnT", [P, DC, TG])
        dtT = sb("dtT", [P, DC, TG])
        uT = sb("uT", [P, DC, TG])
        dA = sb("dA", [P, DC, GB, P])
        hs = sb("hs", [P, DC, TG])
        hC = sb("hC", [P, DC, TG])
        uB = sb("uB", [P, 4, TG])
        uB3b = sb("uB3b", [P, TG])
        bc_sb = sb("bc_sb", [P, 2, 2, TG])
        hm_b = sb("hm_b", [P, TG], BF16)
        hm_c = sb("hm_c", [P, TG], BF16)
        lo_bc = sb("lo_bc", [P, TG], BF16)
        v_sb = sb("v_sb", [P, GB, P])
        negm = sb("negm", [P, GB, P])
        w_gu = sb("w_gu", [P, DC, 2 * NI])
        w_down = sb("w_down", [P, 2, D])
        hT = sb("hT", [P, 2, TG])
        pG = sb("pG", [P, TG])
        th = sb("th", [P, TG])
        pbc = sb("pbc", [P, TG])
        p_t = sb("p_t", [P, GB, NE])
        p_T3 = sb("p_T3", [25, TG], BF16)
        stats = sb("stats", [P, GB, 6])
        mv = sb("mv", [P, GB, 2])
        lnv = sb("lnv", [P, GB])
        rstd = sb("rstd", [P, GB])
        nt = sb("nt", [P, GB])
        mx = sb("mx", [P, HEADS])
        sm = sb("sm", [P, 2, HEADS])
        rs = sb("rs", [P, 2, HEADS])
        lg = sb("lg", [P, GB, E])
        el = sb("el", [P, GB, E])
        gt = sb("gt", [P, GB, E, E])
        eq = sb("eq", [P, GB, E, E])
        rank = sb("rank", [P, GB, E])
        p3b = sb("p3b", [P, GB, 3 * E], BF16)
        p3f = sb("p3f", [P, GB, 3 * E])

        xhat = hC
        xT = hs
        delta = uB[:, 0, :]
        resid = uB[:, 1, :]
        midb = uB[:, 2, :].bitcast(BF16)[:, 0:TG]
        yT = uT
        x1T, aoT = xnT, xnT
        qT, kT = dtT, uT
        k_one = uB3b[:, :]
        ctxT_f = dA[:, :, :, :].rearrange("p c b t -> p c (b t)")
        probs = [t[:, :, :].rearrange("p j (c k) -> p j c k", c=KV) for t in (hs, hC)]
        bias = uB[:, :, :].rearrange("p j (c k) -> p j c k", c=KV)
        pT = bc_sb[:, :, :, :].rearrange("p a b t -> p (a b) t")

        def ub3(n2):
            return uB[:, 3, :] if n2 == 0 else uB3b[:, :]

        ps = ctx.enter_context(nc.psum_tensor("ps", [P, 8, 512], F32))

        def bank(k):
            return ps[:, k, :]

        weights_in = sem("weights_in")
        gpconst = sem("gpconst")
        consts = sem("consts")
        a_exp = sem("a_exp")
        x_in = sem("x_in")
        ctx_in = sem("ctx_in")
        gu_in = sem("gu_in")
        down_in = sem("down_in")
        stored = sem("stored")
        dve_link = sem("dve_link")
        act_link = sem("act_link")
        ln_var = sem("ln_var")
        ln_seed = sem("ln_seed")
        xhat_done = sem("xhat_done")
        xhT_ready = sem("xhT_ready")
        xT_ready = sem("xT_ready")
        xn_done = sem("xn_done")
        xT_done = sem("xT_done")
        proj_ready = sem("proj_ready")
        delta_done = sem("delta_done")
        split_done = sem("split_done")
        z_ready = sem("z_ready")
        z_abs = sem("z_abs")
        z_relu = sem("z_relu")
        z_log = sem("z_log")
        u_done = sem("u_done")
        y_init = sem("y_init")
        b_ready = sem("b_ready")
        c_ready = sem("c_ready")
        b_copied = sem("b_copied")
        c_copied = sem("c_copied")
        ub_done = sem("ub_done")
        ub3_done = sem("ub3_done")
        da_ready = sem("da_ready")
        scan_done = sem("scan_done")
        hc_done = sem("hc_done")
        y_added = sem("y_added")
        g_ready = sem("g_ready")
        up_ready = sem("up_ready")
        pb_ready = sem("pb_ready")
        pb_copied = sem("pb_copied")
        pg_done = sem("pg_done")
        th_done = sem("th_done")
        s_done = sem("s_done")
        hT_done = sem("hT_done")
        d_ready = sem("d_ready")
        acc_done = sem("acc_done")
        out_done = sem("out_done")
        y_copied = sem("y_copied")
        cT_ready = sem("cT_ready")
        cT_done = sem("cT_done")
        op_ready = sem("op_ready")
        x_used = sem("x_used")
        x1_done = sem("x1_done")
        x1T_ready = sem("x1T_ready")
        x1T_done = sem("x1T_done")
        q_ready = sem("q_ready")
        q_done = sem("q_done")
        k_ready = sem("k_ready")
        k_done = sem("k_done")
        k_spread = sem("k_spread")
        v_ready = sem("v_ready")
        v_done = sem("v_done")
        negm_done = sem("negm_done")
        bias_done = sem("bias_done")
        s_ready = sem("s_ready")
        s_added = sem("s_added")
        s_shift = sem("s_shift")
        s_exp = sem("s_exp")
        s_rsum = sem("s_rsum")
        s_norm = sem("s_norm")
        pt_ready = sem("pt_ready")
        pt_done = sem("pt_done")
        ao_ready = sem("ao_ready")
        ao_done = sem("ao_done")
        wo_ready = sem("wo_ready")
        wo_used = sem("wo_used")
        x2_done = sem("x2_done")
        x2T_ready = sem("x2T_ready")
        x2T_done = sem("x2T_done")
        lg_ready = sem("lg_ready")
        lg_done = sem("lg_done")
        lg_exp = sem("lg_exp")
        p_done = sem("p_done")
        pT3_ready = sem("pT3_ready")
        pT3_done = sem("pT3_done")

        block = ctx.enter_context(nc.Block())

        NW = 17
        x_g = a["x"].rearrange("(g b) t d -> g t b d", b=GB)
        ctx_g = a["ctx"].rearrange("(g b) t d -> g t b d", b=GB)
        out_g = out.rearrange("(g b) t d -> g t b d", b=GB)

        def fold(w):
            return w.rearrange("(c k) n -> k c n", k=P)

        @block.sync
        def _(sp):
            def load_x(i):
                sp.dma_start(x_raw[:, :, :], x_g[i]).then_inc(x_in, 16)

            def load_ctx(i):
                sp.dma_start(ctx_raw[:, :, :], ctx_g[i]).then_inc(ctx_in, 16)

            def load_gu(f, gate, up):
                sp.wait_ge(up_ready, 2 * f + 1)
                sp.dma_start(w_gu[:, :, 0:NI], gate).then_inc(gu_in, 16)
                sp.dma_start(w_gu[:, :, NI:], up).then_inc(gu_in, 16)

            def load_down(f, down):
                sp.wait_ge(d_ready, 4 * f + 1)
                sp.dma_start(w_down[:, :, :], down).then_inc(down_in, 16)

            def load_shared(f):
                load_gu(f, fold(a["sgate"]), fold(a["sup"]))
                load_down(f, fold(a["sdown"]))

            def load_expert(f, e):
                w = a["gate_up"][e].rearrange("(c k) n -> k c n", k=P)
                load_gu(f, w[:, :, 0:NI], w[:, :, NI:])
                load_down(f, a["down"][e].rearrange("(c k) n -> k c n", k=P))

            load_x(0)
            for dst, src in (
                (w_xproj[:, :, :], fold(a["xprojT"])), (w_dt[:, :], a["dtprojT"][:, :]),
                (chan[:, :, :], a["chan"][:, :, :]),
                (a_neg[:, :, :], a["A_log"].rearrange("(c p) n -> p c n", p=P)),
                (ident[:, :], a["ident"][:, :]), (picks32[:, :, :], a["picks"][:, :, :]),
                (pickp32[:, :], a["pickp"][:, :]), (w_out[:, :, :], fold(a["outT"])),
                (w_q[:, :, :], fold(a["Wq"])), (w_k[:, :, :], fold(a["Wk"])), (w_v[:, :, :], fold(a["Wv"])),
                (w_o[:, :, :], fold(a["Wo"])), (w_router[:, :, :], fold(a["router"])),
                (alibi[:, :, :, :], a["alibi"][:, :, :, :]), (tri[:, :, :], a["tri"][:, :, :]),
                (masks[:, :, :], a["mask"].rearrange("(o b) t -> o b t", o=1).to_broadcast([P, B, P])),
            ):
                sp.dma_start(dst, src).then_inc(weights_in, 16)
            load_ctx(0)
            with sp.Fori(0, GROUPS) as i:
                load_shared(i * NE)
                with sp.Fori(0, E) as e:
                    load_expert(i * NE + 1 + e, e)
                sp.wait_ge(cT_ready, (i + 1) * DC)
                load_ctx((i + 1) % GROUPS)
                sp.wait_ge(x_used, (i + 1) * GB)
                sp.dma_start(x_raw[:, :, :], x_g[(i + 1) % GROUPS]).then_inc(x_in, 16)
                sp.wait_ge(k_done, i + 1)
                for c in range(KV):
                    for j in range(HPG):
                        sp.dma_start(kT[j * DH:(j + 1) * DH, c, :], k_one[c * DH:(c + 1) * DH, :]).then_inc(k_spread, 16)
            load_shared(GROUPS * NE)
            with sp.Fori(0, E) as e:
                load_expert(GROUPS * NE + 1 + e, e)
            sp.wait_ge(x_in, 16 * (GROUPS + 1))
            sp.wait_ge(ctx_in, 16 * (GROUPS + 1))

        @block.tensor
        def _(pe):
            mm = nc.tensor.matmul

            def k_sum(dst, lhs, rhs, n=DC):
                for k in range(n):
                    r = mm(dst, lhs(k), rhs(k), start=(k == 0), stop=(k == n - 1))
                return r

            def turn(src, banks, ready, before=None):
                for c in range(DC):
                    if before:
                        before(c)
                    for b in range(GB):
                        r = nc.tensor.transpose(bank(banks[c])[:, b * P:(b + 1) * P],
                                                src[:, b, c * P:(c + 1) * P], ident[:, :])
                    r.then_inc(ready, 1)

            def ffn_gate(f, e, c):
                if c == 0:
                    pe.wait_ge(acc_done, 4 * f + 1)
                    mm(bank(7), pick_p[:, bass.ds(e, 1)].to_broadcast([25, P]), p_T3[:, :],
                       start=True, stop=True).then_inc(pb_ready, 1)
                    pe.wait_ge(gu_in, 32 * (f + 1))
                else:
                    pe.wait_ge(pg_done, 2 * f + 2)
                k_sum(bank(6), lambda k: w_gu[:, k, c * P:(c + 1) * P],
                      lambda k: x2T[:, k, :]).then_inc(g_ready, 1)

            def ffn_up(f, c):
                if c == 0:
                    pe.wait_ge(pb_copied, f + 1)
                else:
                    pe.wait_ge(hT_done, 2 * f + 2)
                k_sum(bank(7), lambda k: w_gu[:, k, NI + c * P:NI + (c + 1) * P],
                      lambda k: x2T[:, k, :]).then_inc(up_ready, 1)

            def ffn_down(f, b):
                if b == 0:
                    pe.wait_ge(hT_done, 2 * f + 3)
                    pe.wait_ge(down_in, 16 * (f + 1))
                if b >= 2:
                    pe.wait_ge(acc_done, 4 * f + b)
                k_sum(bank(6 + b % 2), lambda k: hT[:, k, b * P:(b + 1) * P],
                      lambda k: w_down[:, k, :], 2).then_inc(d_ready, 1)

            def ffn_piece(f, e, j):
                if j in (0, 2):
                    ffn_gate(f, e, j // 2)
                elif j in (1, 3):
                    ffn_up(f, j // 2)
                else:
                    ffn_down(f, j - 4)

            def spread_b(n, n2):
                c = pick_hm[:, bass.ds(n, 1)].to_broadcast([P, P])
                mm(bank(4 + n2), c, hm_b[:, :], start=True, stop=False)
                mm(bank(4 + n2), pick_lob[:, bass.ds(n, 1)].to_broadcast([P, P]), lo_bc[:, :],
                   start=False, stop=True).then_inc(b_ready, 1)

            def spread_c(n, n2):
                mm(bank(5 - n2), pick_hm[:, bass.ds(n, 1)].to_broadcast([P, P]), hm_c[:, :], start=True, stop=False)
                mm(bank(5 - n2), pick_loc[:, bass.ds(n, 1)].to_broadcast([P, P]), lo_bc[:, :],
                   start=False, stop=True).then_inc(c_ready, 1)

            pe.wait_ge(weights_in, 16 * (NW - 1))
            pe.wait_ge(consts, 3)
            with pe.Fori(0, GROUPS) as i:
                sf = i * NE
                pe.wait_ge(xhat_done, GB * (i + 1))
                turn(xhat, (0, 1, 2, 3), xhT_ready)
                turn(x_raw, (4, 5, 4, 5), xT_ready,
                     lambda c: pe.wait_ge(xT_done, DC * i + c - 1) if c >= 2 else None)
                ffn_piece(sf, 0, 0)
                pe.wait_ge(xn_done, DC * (i + 1))
                k_sum(bank(0), lambda k: w_xproj[:, k, 0:P], lambda k: xnT[:, k, :]).then_inc(proj_ready, 1)
                for v in range(2):
                    k_sum(bank(1 + v), lambda k: w_xproj[:, k, (1 + v) * P:(2 + v) * P],
                          lambda k: xnT[:, k, :]).then_inc(proj_ready, 1)
                ffn_piece(sf, 0, 1)
                pe.wait_ge(delta_done, i + 1)
                pe.wait_ge(xT_done, DC * (i + 1))
                for c, k in enumerate((3, 4, 5, 0)):
                    mm(bank(k), w_dt[:, c * P:(c + 1) * P], delta, start=True, stop=True).then_inc(z_ready, 1)
                ffn_piece(sf, 0, 2)
                pe.wait_ge(split_done, 2 * (i + 1))
                pe.wait_ge(z_abs, DC * (i + 1))
                pe.wait_ge(z_relu, DC * (i + 1))
                for c in range(DC):
                    r = mm(bank(c), d_diag[:, c, :], xT[:, c, :], start=True, stop=False, skip_group_check=True)
                r.then_inc(y_init, 1)
                ffn_piece(sf, 0, 3)
                spread_b(0, 0)
                spread_c(0, 0)
                for j in range(4, 8):
                    ffn_piece(sf, 0, j)
                with pe.Fori(0, E) as e:
                    for j in range(NJ):
                        n = e * NJ + j
                        nn = i * NS + n
                        ffn_piece(sf + 1 + e, e + 1, j)
                        pe.wait_ge(c_copied, nn + 1)
                        spread_b(n + 1, (j + 1) % 2)
                        for c in range(DC):
                            if c == 2:
                                pe.wait_ge(ub_done, 3 * nn + 3)
                                spread_c(n + 1, (j + 1) % 2)
                            pe.wait_ge(hc_done, 4 * nn + c + 6)
                            mm(bank(c), ident[:, :], hC[:, c, :], start=False, stop=False,
                               skip_group_check=True).then_inc(y_added, 1)
                pe.wait_ge(acc_done, 4 * (sf + NE) + 1)
                pe.wait_ge(ctx_in, 16 * (i + 1))
                turn(ctx_raw, (4, 5, 6, 7), cT_ready)
                pe.wait_ge(y_copied, DC * (i + 1))
                for b in range(GB):
                    pe.wait_ge(cT_done, DC * i + b + 1)
                    k_sum(bank(4 + b), lambda k: yT[:, k, b * P:(b + 1) * P],
                          lambda k: w_out[:, k, :]).then_inc(op_ready, 1)
                pe.wait_ge(x_used, GB * (i + 1))
                k_sum(bank(4), lambda k: w_k[:, k, :], lambda k: ctxT_f[:, k, :]).then_inc(k_ready, 1)
                for b in range(GB):
                    r = k_sum(bank(5)[:, b * P:(b + 1) * P], lambda k: ctxT_f[:, k, b * P:(b + 1) * P],
                              lambda k: w_v[:, k, :])
                r.then_inc(v_ready, 1)
                pe.wait_ge(x1_done, GB * (i + 1))
                turn(x1, (0, 1, 2, 3), x1T_ready)
                pe.wait_ge(x1T_done, DC * (i + 1))
                pe.wait_ge(k_done, i + 1)
                pe.wait_ge(v_done, i + 1)
                for c in range(DC):
                    k_sum(bank(4 + c), lambda k: w_q[:, k, c * P:(c + 1) * P],
                          lambda k: x1T[:, k, :]).then_inc(q_ready, 1)

                def scores(b):
                    bb = i * GB + b
                    if b == 0:
                        pe.wait_ge(k_spread, 16 * HEADS * (i + 1))
                        pe.wait_ge(q_done, DC * (i + 1))
                    else:
                        pe.wait_ge(s_added, HPG * bb)
                    for c in range(KV):
                        for j in range(HPG):
                            r = mm(bank(j)[:, c * P:(c + 1) * P], qT[j * DH:(j + 1) * DH, c, b * P:(b + 1) * P],
                                   kT[j * DH:(j + 1) * DH, c, b * P:(b + 1) * P], start=True, stop=True)
                    r.then_inc(s_ready, 1)

                scores(0)
                for b in range(GB):
                    bb = i * GB + b
                    if b + 1 < GB:
                        scores(b + 1)
                    pe.wait_ge(s_norm, bb + 1)
                    for c in range(KV):
                        if c >= 2:
                            pe.wait_ge(pt_done, KV * bb + c - 1)
                        for j in range(HPG):
                            r = nc.tensor.transpose(bank(4 + c % 2)[:, j * P:(j + 1) * P], probs[b % 2][:, j, c, :], ident[:, :])
                        r.then_inc(pt_ready, 1)
                    for c in range(KV):
                        pe.wait_ge(pt_done, KV * bb + c + 1)
                        for j in range(HPG):
                            r = mm(ps[j * DH:(j + 1) * DH, 6, c * P:(c + 1) * P], v_sb[:, b, c * DH:(c + 1) * DH],
                                   pT[:, c, j * P:(j + 1) * P], start=True, stop=True)
                    r.then_inc(ao_ready, 1)
                    pe.wait_ge(ao_done, bb + 1)
                    pe.wait_ge(wo_used, bb + 1)
                    k_sum(bank(7), lambda k: aoT[:, k, b * P:(b + 1) * P], lambda k: w_o[:, k, :]).then_inc(wo_ready, 1)
                pe.wait_ge(x2_done, GB * (i + 1))
                turn(acc, (0, 1, 2, 3), x2T_ready)
                pe.wait_ge(x2T_done, DC * (i + 1))
                for b in range(GB):
                    r = k_sum(bank(4)[:, b * E:(b + 1) * E], lambda k: x2T[:, k, b * P:(b + 1) * P],
                              lambda k: w_router[:, k, :])
                r.then_inc(lg_ready, 1)
                pe.wait_ge(p_done, i + 1)
                for b in range(GB):
                    r = nc.tensor.transpose(bank(5)[0:3 * E, b * P:(b + 1) * P], p3f[:, b, :], ident[:, :])
                r.then_inc(pT3_ready, 1)
                pe.wait_ge(pT3_done, i + 1)
            for j in range(8):
                ffn_piece(GROUPS * NE, 0, j)
            with pe.Fori(0, E) as e:
                for j in range(8):
                    ffn_piece(GROUPS * NE + 1 + e, e + 1, j)

        @block.scalar
        def _(act):
            act_fn = nc.scalar.activation

            class Link:
                def __init__(self):
                    self.base, self.n = 0, 0

                def __call__(self, ins):
                    ins.then_inc(act_link, 1)
                    self.n += 1

                def wait(self):
                    act.wait_ge(act_link, self.base + self.n)

            link = Link()

            def ln_seeds(ln):
                act.wait_ge(ln_var, ln + 1)
                link(act_fn(lnv[:, :], mv[:, :, 1], ACT.Ln))
                link.wait()
                act_fn(rstd[:, :], lnv[:, :], ACT.Exp, scale=-0.5).then_inc(ln_seed, 1)

            def ffn_copy(f):
                act.wait_ge(pb_ready, f + 1)
                act.wait_ge(pg_done, 2 * f + 1)
                act_fn(pbc[:, :], bank(7), ACT.Copy).then_inc(pb_copied, 1)

            def ffn_tanh(f, c):
                act.wait_ge(pg_done, 2 * f + c + 2)
                act.wait_ge(hT_done, 2 * f + c + 1)
                act_fn(th[:, :], pG[:, :], ACT.Tanh, scale=0.5).then_inc(th_done, 1)

            def exps(i, n, c):
                nn = i * NS + n
                act.wait_ge(scan_done, 4 * nn + c + 2)
                act_fn(dA[:, c, :, 1:P], dtT[:, c, :].rearrange("p (b t) -> p b t", b=GB)[:, :, 1:P], ACT.Exp,
                       scale=a_neg[:, c, bass.ds(n, 1)]).then_inc(da_ready, 1)

            act.wait_ge(weights_in, 16 * (NW - 1))
            act_fn(a_neg[:, :, :], a_neg[:, :, :], ACT.Exp).then_inc(a_exp, 1)
            act.wait_ge(consts, 3)
            with act.Fori(0, GROUPS) as i:
                link.base, link.n = i * ACT_LINKS, 0
                sf = i * NE
                ln_seeds(LN_PASS * i)
                for c in range(DC):
                    act.wait_ge(xhT_ready, DC * i + c + 1)
                    act_fn(xnT[:, c, :], bank(c), ACT.Identity, scale=chan[:, 0, c:c + 1],
                           bias=chan[:, 1, c:c + 1]).then_inc(xn_done, 1)
                ffn_copy(sf)
                act.wait_ge(proj_ready, 3 * i + 1)
                act_fn(delta, bank(0), ACT.Copy).then_inc(delta_done, 1)
                ffn_tanh(sf, 0)
                for c, k in enumerate((3, 4, 5, 0)):
                    act.wait_ge(z_ready, DC * i + c + 1)
                    act_fn(dtT[:, c, :], bank(k), ACT.Abs, bias=chan[:, 2, c:c + 1]).then_inc(z_abs, 1)
                ffn_tanh(sf, 1)
                act.wait_ge(z_abs, DC * (i + 1))
                for c in range(DC):
                    link(act_fn(dtT[:, c, :], dtT[:, c, :], ACT.Exp, scale=-1.0))
                link.wait()
                for c in range(DC):
                    act_fn(dtT[:, c, :], dtT[:, c, :], ACT.Ln, bias=1.0).then_inc(z_log, 1)
                act.wait_ge(u_done, i + 1)
                with act.Fori(0, E) as e:
                    for j in range(NJ):
                        f = sf + 1 + e
                        n = e * NJ + j
                        nn = i * NS + n
                        act.wait_ge(b_ready, i * (NS + 1) + n + 1)
                        act.wait_ge(ub3_done, nn + 1)
                        act_fn(bc_sb[:, 0, j % 2, :], bank(4 + j % 2), ACT.Copy).then_inc(b_copied, 1)
                        exps(i, n, 0)
                        exps(i, n, 1)
                        act.wait_ge(c_ready, i * (NS + 1) + n + 1)
                        act.wait_ge(hc_done, 4 * nn + 1)
                        act_fn(bc_sb[:, 1, j % 2, :], bank(5 - j % 2), ACT.Copy).then_inc(c_copied, 1)
                        if j in (1, 3):
                            ffn_tanh(f, j // 2)
                        exps(i, n, 2)
                        exps(i, n, 3)
                        if j == 0:
                            ffn_copy(f)
                act.wait_ge(y_added, 4 * NS * (i + 1) + 4)
                act.wait_ge(scan_done, 4 * NS * (i + 1) + 5)
                act.wait_ge(ub3_done, NS * (i + 1) + 2)
                for c in range(DC):
                    act_fn(yT[:, c, :], bank(c), ACT.Copy).then_inc(y_copied, 1)
                ln_seeds(LN_PASS * i + 1)
                ln_seeds(LN_PASS * i + 2)
                for c in range(DC):
                    act.wait_ge(x1T_ready, DC * i + c + 1)
                    act_fn(x1T[:, c, :], bank(c), ACT.Copy).then_inc(x1T_done, 1)
                for c in range(DC):
                    act.wait_ge(q_ready, DC * i + c + 1)
                    act_fn(qT[:, c, :], bank(4 + c), ACT.Copy, scale=float(1.0 / np.sqrt(DH))).then_inc(q_done, 1)

                def softmax_exp(b):
                    bb = i * GB + b
                    act.wait_ge(s_shift, bb + 1)
                    act_fn(probs[b % 2], probs[b % 2], ACT.Exp).then_inc(s_exp, 1)

                softmax_exp(0)
                for b in range(GB):
                    bb = i * GB + b
                    if b + 1 < GB and b < 1:
                        softmax_exp(b + 1)
                    for c in range(KV):
                        act.wait_ge(pt_ready, KV * bb + c + 1)
                        act.wait_ge(ao_ready, bb + 1)
                        act_fn(pT[:, c, :], bank(4 + c % 2), ACT.Copy).then_inc(pt_done, 1)
                    if 1 <= b and b + 1 < GB:
                        softmax_exp(b + 1)
                    act.wait_ge(ao_ready, bb + 2)
                    act_fn(aoT[:, :, b * P:(b + 1) * P], bank(6).rearrange("p (c q) -> p c q", c=KV),
                           ACT.Copy).then_inc(ao_done, 1)
                ln_seeds(LN_PASS * i + 3)
                for c in range(DC):
                    act.wait_ge(x2T_ready, DC * i + c + 1)
                    act_fn(x2T[:, c, :], bank(c), ACT.Copy).then_inc(x2T_done, 1)
                act.wait_ge(lg_done, i + 1)
                act_fn(el[:, :, :], lg[:, :, :], ACT.Exp, scale=-1.0).then_inc(lg_exp, 1)
                act.wait_ge(pT3_ready, i + 1)
                act_fn(p_T3[0:3 * E, :], bank(5)[0:3 * E, :], ACT.Copy).then_inc(pT3_done, 1)
                assert link.n == ACT_LINKS, link.n
            link.base, link.n = GROUPS * (ACT_LINKS), 0
            ffn_copy(GROUPS * NE)
            ffn_tanh(GROUPS * NE, 0)
            ffn_tanh(GROUPS * NE, 1)
            with act.Fori(0, E) as e:
                f = GROUPS * NE + 1 + e
                ffn_copy(f)
                ffn_tanh(f, 0)
                ffn_tanh(f, 1)
            ln_seeds(LN_PASS * GROUPS)

        @block.vector
        def _(dve):
            v = nc.vector

            class Link:
                def __init__(self):
                    self.base, self.n = 0, 0

                def __call__(self, ins):
                    ins.then_inc(dve_link, 1)
                    self.n += 1
                    dve.wait_ge(dve_link, self.base + self.n)

            link = Link()

            def norm(ln, src, dst, done):
                for b in range(GB):
                    last = v.bn_stats(stats[:, b, :], src[:, b, :])
                link(last)
                v.memset(nt[:, :], 0.0)
                for b in range(GB):
                    last = v.bn_aggr(mv[:, b, :], stats[:, b, :])
                link(last)
                v.tensor_scalar(mv[:, :, 1], mv[:, :, 1], EPS, None, ALU.add).then_inc(ln_var, 1)
                dve.wait_ge(ln_seed, ln + 1)
                link(v.tensor_tensor(nt[:, :], rstd[:, :], rstd[:, :], ALU.mult))
                link(v.tensor_tensor(nt[:, :], nt[:, :], mv[:, :, 1], ALU.mult))
                link(v.tensor_scalar(nt[:, :], nt[:, :], -0.5, 1.5, ALU.mult, ALU.add))
                link(v.tensor_tensor(rstd[:, :], rstd[:, :], nt[:, :], ALU.mult))
                for b in range(GB):
                    v.tensor_scalar(dst[:, b, :], src[:, b, :], mv[:, b, 0:1], rstd[:, b:b + 1],
                                    ALU.subtract, ALU.mult).then_inc(done, 1)

            def ffn_pg(f, c):
                dve.wait_ge(g_ready, 2 * f + c + 1)
                dve.wait_ge(pb_copied, f + 1)
                v.tensor_tensor(pG[:, :], bank(6), pbc[:, :], ALU.mult).then_inc(pg_done, 1)

            def ffn_h(f, c):
                dve.wait_ge(th_done, 2 * f + c + 1)
                v.scalar_tensor_tensor(th[:, :], th[:, :], 1.0, pG[:, :], ALU.add, ALU.mult).then_inc(s_done, 1)
                dve.wait_ge(s_done, 2 * f + c + 1)
                dve.wait_ge(up_ready, 2 * f + c + 2)
                v.scalar_tensor_tensor(hT[:, c, :], th[:, :], 0.5, bank(7), ALU.mult, ALU.mult).then_inc(hT_done, 1)

            def ffn_acc(f, e, b):
                dve.wait_ge(d_ready, 4 * f + b + 2)
                v.scalar_tensor_tensor(acc[:, b, :], bank(6 + b % 2), p_t[:, b, bass.ds(e, 1)], acc[:, b, :],
                                       ALU.mult, ALU.add).then_inc(acc_done, 1)

            def ffn_piece(f, e, j):
                if j in (0, 2):
                    ffn_pg(f, j // 2)
                elif j in (1, 3):
                    ffn_h(f, j // 2)
                else:
                    ffn_acc(f, e, j - 4)

            v.memset(x2T[:, :, :], 0.0)
            v.memset(acc[:, :, :], 0.0)
            v.memset(p_t[:, :, :], 1.0)
            v.memset(p_T3[:, :], 1.0).then_inc(consts, 1)
            for k, free in enumerate((up_ready, d_ready, acc_done, pg_done, hT_done, ao_ready, wo_used)):
                v.memset(mx[:, k:k + 1], 0.0).then_inc(free, 1)
            v.memset(dA[:, :, :, :], 0.0).then_inc(scan_done, 5)
            dve.wait_ge(weights_in, 16 * (NW - 1))
            v.tensor_copy(pick_hm[:, :], picks32[:, 0, :])
            v.tensor_copy(pick_lob[:, :], picks32[:, 1, :])
            v.tensor_copy(pick_loc[:, :], picks32[:, 2, :])
            v.tensor_copy(pick_p[:, :], pickp32[:, :])
            for c in range(DC):
                v.tensor_scalar(d_diag[:, c, :], ident[:, :], chan[:, 3, c:c + 1], None, ALU.mult)
            v.tensor_copy(identb[:, :], ident[:, :]).then_inc(consts, 1)
            dve.wait_ge(y_added, 4)
            dve.wait_ge(hc_done, 5)
            dve.wait_ge(a_exp, 1)
            v.tensor_scalar(a_neg[:, :, :], a_neg[:, :, :], -1.0, None, ALU.mult).then_inc(consts, 1)
            dve.wait_ge(consts, 3)

            with dve.Fori(0, GROUPS) as i:
                link.base, link.n = i * DVE_LINKS, 0
                sf = i * NE
                dve.wait_ge(x_in, 16 * (i + 1))
                norm(LN_PASS * i, x_raw, xhat, xhat_done)
                link(v.memset(dA[:, :, :, 0:1], 0.0))
                for c in range(DC):
                    dve.wait_ge(xT_ready, DC * i + c + 1)
                    v.tensor_copy(xT[:, c, :], bank(4 + c % 2)).then_inc(xT_done, 1)
                ffn_piece(sf, 0, 0)
                for m, (hm, lo) in enumerate(((hm_b, slice(0, NS)), (hm_c, slice(NS, P)))):
                    dve.wait_ge(proj_ready, 3 * i + 2 + m)
                    link(v.tensor_copy(hm[:, :], bank(1 + m)))
                    link(v.tensor_tensor(resid, bank(1 + m), hm[:, :], ALU.subtract))
                    link(v.tensor_copy(midb, resid))
                    v.tensor_copy(hm[NS:P, :], midb[NS:P, :])
                    v.tensor_tensor(lo_bc[lo, :], resid[lo, :], midb[lo, :], ALU.subtract).then_inc(split_done, 1)
                    dve.wait_ge(split_done, 2 * i + m + 1)
                ffn_piece(sf, 8, 1)
                for c, k in enumerate((3, 4, 5, 0)):
                    dve.wait_ge(z_abs, DC * i + c + 1)
                    v.tensor_scalar(uT[:, c, :], bank(k), chan[:, 2, c:c + 1], 0.0, ALU.add,
                                    ALU.max).then_inc(z_relu, 1)
                ffn_piece(sf, 0, 2)
                ffn_piece(sf, 0, 3)
                for c in range(DC):
                    dve.wait_ge(z_log, DC * i + c + 1)
                    dve.wait_ge(z_relu, DC * i + c + 1)
                    link(v.tensor_tensor(dtT[:, c, :], dtT[:, c, :], uT[:, c, :], ALU.add))
                    last = v.tensor_tensor(uT[:, c, :], dtT[:, c, :], xnT[:, c, :], ALU.mult)
                last.then_inc(u_done, 1)
                dve.wait_ge(u_done, i + 1)
                dve.wait_ge(y_init, i + 1)
                for j in range(4, 8):
                    ffn_piece(sf, 8, j)
                with dve.Fori(0, E) as e:
                    for j in range(NJ):
                        f = sf + 1 + e
                        nn = i * NS + e * NJ + j
                        dve.wait_ge(b_copied, nn + 1)
                        for c in range(3):
                            dve.wait_ge(scan_done, 4 * nn + c + 2)
                            ins = v.tensor_tensor(uB[:, c, :], uT[:, c, :], bank(4 + j % 2), ALU.mult)
                            ins.then_inc(ub_done, 1)
                            if c == 2:
                                dve.wait_ge(ub_done, 3 * nn + 1)
                        for c in range(DC):
                            if c == 1:
                                dve.wait_ge(ub_done, 3 * nn + 3)
                            src = uB[:, c, :] if c < 3 else ub3(j % 2)
                            if c == 3:
                                dve.wait_ge(ub3_done, nn + 3)
                            dve.wait_ge(da_ready, 4 * nn + c + 1)
                            dve.wait_ge(hc_done, 4 * nn + c + 2)
                            v.tensor_tensor_scan(hs[:, c, :], dA[:, c, :, :].rearrange("p b t -> p (b t)"), src,
                                                 0.0, ALU.mult, ALU.add).then_inc(scan_done, 1)
                        ffn_piece(f, e, j)
                link(v.memset(nt[:, :], 0.0))
                norm(LN_PASS * i + 1, acc, acc, out_done)
                for c in range(DC):
                    dve.wait_ge(cT_ready, DC * i + c + 1)
                    v.tensor_copy(ctxT_f[:, c, :], bank(4 + c)).then_inc(cT_done, 1)
                for b in range(GB):
                    dve.wait_ge(op_ready, GB * i + b + 1)
                    v.tensor_tensor(x1[:, b, :], bank(4 + b), x_raw[:, b, :], ALU.add).then_inc(x_used, 1)
                dve.wait_ge(x_used, GB * (i + 1))
                dve.wait_ge(k_ready, i + 1)
                v.tensor_copy(k_one, bank(4)).then_inc(k_done, 1)
                dve.wait_ge(v_ready, i + 1)
                v.tensor_copy(v_sb[:, :, :].rearrange("p b n -> p (b n)"), bank(5)).then_inc(v_done, 1)
                norm(LN_PASS * i + 2, x1, x1, x1_done)
                v.tensor_scalar(negm[:, :, :], masks[:, bass.ds(i * GB, GB), :], -NEG, NEG,
                                ALU.mult, ALU.add).then_inc(negm_done, 1)

                def shift(b):
                    bb = i * GB + b
                    p4 = probs[b % 2]
                    dve.wait_ge(s_ready, bb + 1)
                    dve.wait_ge(bias_done, bb + 1)
                    if b >= 2:
                        dve.wait_ge(pt_ready, KV * (bb - 1))
                    for j in range(HPG):
                        v.tensor_tensor(p4[:, j, :, :], bank(j).rearrange("p (c k) -> p c k", c=KV),
                                        bias[:, j, :, :], ALU.add).then_inc(s_added, 1)
                    dve.wait_ge(s_added, HPG * (bb + 1))
                    p3 = p4.rearrange("p j c k -> p (j c) k")
                    link(v.tensor_reduce(mx[:, :], p3, AX.X, ALU.max))
                    v.tensor_tensor(p3, p3, mx[:, :].unsqueeze(2).to_broadcast([P, HEADS, P]),
                                    ALU.subtract).then_inc(s_shift, 1)

                def row_sums(b):
                    bb = i * GB + b
                    p3 = probs[b % 2].rearrange("p j c k -> p (j c) k")
                    dve.wait_ge(s_exp, bb + 1)
                    link(v.tensor_reduce(sm[:, b % 2, :], p3, AX.X, ALU.add))
                    v.reciprocal(rs[:, b % 2, :], sm[:, b % 2, :]).then_inc(s_rsum, 1)

                def residual(b):
                    bb = i * GB + b
                    dve.wait_ge(wo_ready, bb + 1)
                    dve.wait_ge(stored, 16 * (i + 1))
                    v.tensor_tensor(acc[:, b, :], bank(7), x1[:, b, :], ALU.add).then_inc(wo_used, 1)

                shift(0)
                for b in range(GB):
                    row_sums(b)
                    if b == 0:
                        shift(1)
                    elif b + 1 < GB:
                        shift(b + 1)
                        residual(b - 1)
                residual(2)
                residual(3)
                dve.wait_ge(wo_used, GB * (i + 1) + 1)
                norm(LN_PASS * i + 3, acc, acc, x2_done)
                dve.wait_ge(lg_ready, i + 1)
                v.tensor_copy(lg[:, :, :].rearrange("p b e -> p (b e)"), bank(4)[:, 0:GB * E]).then_inc(lg_done, 1)
                dve.wait_ge(lg_done, i + 1)
                other = lg[:, :, :].unsqueeze(2).to_broadcast([P, GB, E, E])
                own = lg[:, :, :].unsqueeze(3).to_broadcast([P, GB, E, E])
                v.tensor_tensor(gt[:, :, :, :], other, own, ALU.is_gt)
                link(v.tensor_tensor(eq[:, :, :, :], other, own, ALU.is_equal))
                link(v.tensor_tensor(eq[:, :, :, :], eq[:, :, :, :],
                                     tri[:, :, :].unsqueeze(1).to_broadcast([P, GB, E, E]), ALU.mult))
                link(v.tensor_tensor(gt[:, :, :, :], gt[:, :, :, :], eq[:, :, :, :], ALU.add))
                link(v.tensor_reduce(rank[:, :, :].rearrange("p b e -> p (b e)"),
                                     gt[:, :, :, :].rearrange("p b e o -> p (b e) o"), AX.X, ALU.add))
                dve.wait_ge(lg_exp, i + 1)
                link(v.tensor_scalar(el[:, :, :], el[:, :, :], 1.0, None, ALU.add))
                link(v.reciprocal(el[:, :, :], el[:, :, :]))
                link(v.scalar_tensor_tensor(p_t[:, :, 0:E], rank[:, :, :], 2.0, el[:, :, :], ALU.is_lt, ALU.mult))
                link(v.tensor_copy(p3b[:, :, 0:E], p_t[:, :, 0:E]))
                link(v.tensor_tensor(el[:, :, :], p_t[:, :, 0:E], p3b[:, :, 0:E], ALU.subtract))
                link(v.tensor_copy(p3b[:, :, E:2 * E], el[:, :, :]))
                link(v.tensor_tensor(p3b[:, :, 2 * E:], el[:, :, :], p3b[:, :, E:2 * E], ALU.subtract))
                v.tensor_copy(p3f[:, :, :], p3b[:, :, :]).then_inc(p_done, 1)
                assert link.n == DVE_LINKS, link.n
            link.base, link.n = GROUPS * DVE_LINKS, 0
            for j in range(8):
                ffn_piece(GROUPS * NE, 8, j)
            with dve.Fori(0, E) as e:
                for j in range(8):
                    ffn_piece(GROUPS * NE + 1 + e, e, j)
            dve.wait_ge(acc_done, 4 * NE * (GROUPS + 1) + 1)
            norm(LN_PASS * GROUPS, acc, acc, out_done)

        @block.gpsimd
        def _(pool):
            g = nc.gpsimd
            g.memset(hC[:, :, :], 0.0).then_inc(y_added, 4)
            g.memset(hs[:, :, :], 0.0).then_inc(hc_done, 5)
            g.memset(uB3b[:, :], 0.0).then_inc(ub3_done, 2)
            pool.wait_ge(weights_in, 16 * (NW - 1))
            with pool.Fori(0, GROUPS) as i:
                with pool.Fori(0, E) as e:
                    for j in range(NJ):
                        nn = i * NS + e * NJ + j
                        if j == 0:
                            pool.wait_ge(u_done, i + 1)
                        pool.wait_ge(b_copied, nn + 1)
                        pool.wait_ge(scan_done, 4 * nn + 1)
                        g.tensor_tensor(ub3(j % 2), uT[:, 3, :], bc_sb[:, 0, j % 2, :], ALU.mult).then_inc(ub3_done, 1)
                        pool.wait_ge(c_copied, nn + 1)
                        for c in range(DC):
                            pool.wait_ge(scan_done, 4 * nn + c + 6)
                            pool.wait_ge(y_added, 4 * nn + c + 1)
                            g.tensor_tensor(hC[:, c, :], hs[:, c, :], bc_sb[:, 1, j % 2, :],
                                            ALU.mult).then_inc(hc_done, 1)
                pool.wait_ge(out_done, GB * (i + 1))
                pool.dma_start(out_g[(i + GROUPS - 1) % GROUPS], acc[:, :, :]).then_inc(stored, 16)

                def add_bias(b):
                    g.tensor_tensor(bias, alibi[:, :, :, :],
                                    negm[:, b, :].unsqueeze(1).unsqueeze(1).to_broadcast([P, HPG, KV, P]),
                                    ALU.add).then_inc(bias_done, 1)

                pool.wait_ge(negm_done, i + 1)
                add_bias(0)
                for b in range(GB):
                    bb = i * GB + b
                    if b + 1 < GB:
                        pool.wait_ge(s_added, HPG * (bb + 1))
                        add_bias(b + 1)
                    pool.wait_ge(s_rsum, bb + 1)
                    p3 = probs[b % 2].rearrange("p j c k -> p (j c) k")
                    g.tensor_tensor(p3, p3, rs[:, b % 2, :].unsqueeze(2).to_broadcast([P, HEADS, P]),
                                    ALU.mult).then_inc(s_norm, 1)
            pool.wait_ge(out_done, GB * (GROUPS + 1))
            pool.dma_start(out_g[GROUPS - 1], acc[:, :, :]).then_inc(stored, 16)
            pool.wait_ge(stored, 16 * (GROUPS + 1))


def kernel(**inputs):
    import concourse.bacc as bacc
    from concourse.bass_utils import run_bass_kernel_spmd

    def arr(name):
        return np.asarray(inputs[name])

    picks = np.zeros((P, 3, NS + 1), np.float32)
    for n in range(NS):
        picks[n, 0, n] = picks[NS + n, 0, n] = 1
        picks[n, 1, n] = picks[NS + n, 2, n] = 1
    pickp = np.zeros((25, NE), np.float32)
    pickp[24, 0] = 1
    for e in range(E):
        pickp[[e, E + e, 2 * E + e], 1 + e] = 1
    m0 = np.float32(2.0 ** (-8.0 / HEADS))
    slopes = (m0 ** np.arange(1, HEADS + 1, dtype=np.float32)).reshape(KV, HPG).T
    rel = np.arange(P, dtype=np.float32)[None, :] - np.arange(P, dtype=np.float32)[:, None]
    alibi = slopes[None, :, :, None] * rel[:, None, None, :]
    tri = np.broadcast_to(np.tril(np.ones((E, E), np.float32), -1), (P, E, E))
    xproj = arr("L0_attn_x_proj_w")
    rows = [*range(P), *(2 * [*range(P, P + NS)]), *(2 * [*range(P + NS, P + 2 * NS)])]
    arrays = {
        "x": arr("x"), "ctx": arr("ctx_2048"), "mask": arr("mask_BxS2_bf1").view(np.uint8),
        "chan": np.stack([arr("L0_attn_norm_w"), arr("L0_attn_norm_b"), arr("L0_attn_dt_proj_b"),
                          arr("L0_attn_D_param")]).reshape(4, DC, P).transpose(2, 0, 1),
        "xprojT": xproj[rows].T, "dtprojT": arr("L0_attn_dt_proj_w").T,
        "A_log": arr("L0_attn_A_log"), "outT": arr("L0_attn_out_proj_w").T,
        "Wq": arr("L0_xattn_Wq"), "Wk": arr("L0_xattn_Wk"), "Wv": arr("L0_xattn_Wv"), "Wo": arr("L0_xattn_Wo"),
        "router": arr("L0_ffn_router_w"), "gate_up": arr("L0_ffn_gate_up_w"), "down": arr("L0_ffn_down_w"),
        "sgate": arr("L0_ffn_shared_gate_w"), "sup": arr("L0_ffn_shared_up_w"), "sdown": arr("L0_ffn_shared_down_w"),
        "ident": np.eye(P, dtype=np.float32), "picks": picks, "pickp": pickp,
        "alibi": alibi.astype(np.float32), "tri": tri,
    }
    nc = bacc.Bacc("TRN2", target_bir_lowering=False, num_devices=1)
    feed, aps = {}, {}
    for name, v in arrays.items():
        v = np.ascontiguousarray(v)
        feed[f"in_{name}"] = v
        aps[name] = nc.dram_tensor(f"in_{name}", v.shape, mybir.dt.from_np(v.dtype), kind="ExternalInput").ap()
    out = nc.dram_tensor("out", (B, P, D), F32, kind="ExternalOutput").ap()
    decoder_layer_kernel(nc, aps, out)
    r = run_bass_kernel_spmd(nc, [feed], core_ids=[0])
    return r.results[0]["out"]
```

```python
from contextlib import ExitStack

import numpy as np

import concourse.bass as bass
from concourse import mybir

ALU = mybir.AluOpType
ACT = mybir.ActivationFunctionType
AX = mybir.AxisListType
F32 = mybir.dt.float32
F32R = mybir.dt.float32r
I32 = mybir.dt.int32
BF16 = mybir.dt.bfloat16
U8 = mybir.dt.uint8

P = 128
B = 32
GB = 4
TG = GB * P
GROUPS = B // GB
D = 512
DC = D // P
NS = 64
NJ = 8
E = 8
NI = 256
NE = E + 1
HEADS = 16
KV = 4
HPG = HEADS // KV
DH = D // HEADS
EPS = 1e-5
RSQRT_SEED = 0x5F3759DF
NEG = float(np.finfo(np.float32).min)



def decoder_layer_kernel(nc, a, out):
    ctx = ExitStack()
    with ctx:
        def sb(name, shape, dt=F32):
            return ctx.enter_context(nc.sbuf_tensor(name, shape, dt))

        def sem(name):
            return ctx.enter_context(nc.semaphore(name))

        w_xproj = sb("w_xproj", [P, DC, P + 2 * NS])
        w_dt = sb("w_dt", [P, D])
        w_out = sb("w_out", [P, DC, D])
        w_q = sb("w_q", [P, DC, D])
        w_k = sb("w_k", [P, DC, P])
        w_v = sb("w_v", [P, DC, P])
        w_o = sb("w_o", [P, DC, D])
        w_router = sb("w_router", [P, 2, DC, E], F32R)
        router32 = sb("router32", [P, DC, E])
        chan = sb("chan", [P, 4, DC])
        a_neg = sb("a_neg", [P, DC, NS])
        d_diag = sb("d_diag", [P, DC, P])
        ident = sb("ident", [P, P])
        pick_bc = sb("pick_bc", [3 * NJ, NJ], BF16)
        pick_p = sb("pick_p", [25, NE], BF16)
        pickb32 = sb("pickb32", [3 * NJ, NJ])
        pickp32 = sb("pickp32", [25, NE])
        alibi = sb("alibi", [P, HPG, KV, P])
        tri = sb("tri", [P, E, E])
        masks = sb("masks", [P, GB, P], U8)

        x_raw = sb("x_raw", [P, GB, D])
        x1 = sb("x1", [P, GB, D])
        acc = sb("acc", [P, GB, D])
        x2T = sb("x2T", [P, 2, DC, TG], F32R)
        xnT = sb("xnT", [P, DC, TG])
        dtT = sb("dtT", [P, DC, TG])
        uT = sb("uT", [P, DC, TG])
        dA = sb("dA", [P, DC, GB, P])
        hs = sb("hs", [P, DC, TG])
        hC = sb("hC", [P, DC, TG])
        uB = sb("uB", [P, 4, TG])
        uB3b = sb("uB3b", [P, TG])
        bc_sb = sb("bc_sb", [P, 2, 2, TG])
        bc_parts = sb("bc_parts", [P, 3, TG], BF16)
        stage = sb("stage", [3 * NJ, 2, 2, TG], BF16)
        k_one = sb("k_one", [P, TG])
        v_sb = sb("v_sb", [P, GB, KV, DH + 1])
        negm = sb("negm", [P, GB, P])
        w_gu = sb("w_gu", [P, 2, DC, 2 * NI], F32R)
        w_down = sb("w_down", [P, 2, 2, D], F32R)
        hT = sb("hT", [P, 2, 2, TG], F32R)
        pG = sb("pG", [P, TG])
        th = sb("th", [P, TG])
        pbc = sb("pbc", [P, TG])
        p_t = sb("p_t", [P, GB, NE])
        p_T3 = sb("p_T3", [25, TG], BF16)
        stats = sb("stats", [P, GB, 6])
        mv = sb("mv", [P, GB, 2])
        rstd = sb("rstd", [P, GB])
        rseed = sb("rseed", [P, GB], I32)
        nt = sb("nt", [P, GB])
        mx = sb("mx", [P, 2, HEADS])
        rs = sb("rs", [P, HEADS])
        sums = sb("sums", [P, HEADS])
        lg = sb("lg", [P, GB, E])
        el = sb("el", [P, GB, E])
        rank = sb("rank", [P, GB, E])
        p3b = sb("p3b", [P, GB, 3 * E], BF16)
        p3f = sb("p3f", [P, GB, 3 * E])

        xhat = hC
        xT = hs
        delta = uB[:, 0, :]
        resid = uB[:, 1, :]
        yT, qT, ctxT = dtT, dtT, dtT
        kT = uT
        x1T, aoT = xnT, xnT
        ctx_raw = dA[:, :, :, :].rearrange("p c b t -> p c (b t)")
        probs = [t[:, :, :].rearrange("p j (c k) -> p j c k", c=KV) for t in (hs, hC)]
        bias = uB[:, :, :].rearrange("p j (c k) -> p j c k", c=KV)
        pT = bc_sb[:, :, :, :].rearrange("p a b t -> p (a b) t")
        ao_q = uB3b
        split_in = [pG, th]
        gt, eq = (pbc[:, m * TG // 2:(m + 1) * TG // 2].rearrange("p (b e o) -> p b e o", b=GB, e=E) for m in range(2))

        def ub3(n2):
            return uB[:, 3, :] if n2 == 0 else uB3b[:, :]

        ps = ctx.enter_context(nc.psum_tensor("ps", [P, 8, 512], F32))

        def bank(k):
            return ps[:, k, :]

        gu_parts = nc.dram_tensor("gu_parts", [NE, P, 2, DC, 2 * NI], F32, kind="Internal").ap()
        down_parts = nc.dram_tensor("down_parts", [NE, P, 2, 2, D], F32, kind="Internal").ap()
        bc_dram = nc.dram_tensor("bc_dram", [2 * NS, 3, TG], BF16, kind="Internal").ap()

        weights_in = sem("weights_in")
        consts = sem("consts")
        a_exp = sem("a_exp")
        wsplit_in = [sem("wsplit_even_in"), sem("wsplit_odd_in")]
        wsplit_done = sem("wsplit_done")
        wsplit_high = sem("wsplit_high")
        gu_out = sem("gu_out")
        down_out = sem("down_out")
        x_in = sem("x_in")
        ctx_in = sem("ctx_in")
        mask_in = sem("mask_in")
        gu_in = sem("gu_in")
        down_in = sem("down_in")
        bc_out = sem("bc_out")
        stage_in = sem("stage_in")
        stored = sem("stored")
        dve_link = sem("dve_link")
        ln_link = sem("ln_link")
        act_link = sem("act_link")
        xhat_done = sem("xhat_done")
        xhT_ready = sem("xhT_ready")
        xT_ready = sem("xT_ready")
        xn_done = sem("xn_done")
        xT_done = sem("xT_done")
        cT_ready = sem("cT_ready")
        cT_done = sem("cT_done")
        k_ready = sem("k_ready")
        k_done = sem("k_done")
        k_spread = sem("k_spread")
        v_ready = sem("v_ready")
        v_done = sem("v_done")
        proj_ready = sem("proj_ready")
        delta_done = sem("delta_done")
        split_done = sem("split_done")
        z_ready = sem("z_ready")
        z_abs = sem("z_abs")
        z_relu = sem("z_relu")
        z_log = sem("z_log")
        u_done = sem("u_done")
        y_init = sem("y_init")
        b_ready = sem("b_ready")
        c_ready = sem("c_ready")
        b_copied = sem("b_copied")
        c_copied = sem("c_copied")
        ub_done = sem("ub_done")
        ub3_done = sem("ub3_done")
        da_ready = sem("da_ready")
        scan_done = sem("scan_done")
        hc_done = sem("hc_done")
        y_added = sem("y_added")
        g_ready = sem("g_ready")
        up_ready = sem("up_ready")
        pb_ready = sem("pb_ready")
        pb_copied = sem("pb_copied")
        pg_done = sem("pg_done")
        th_done = sem("th_done")
        s_done = sem("s_done")
        h_done = sem("h_done")
        hh_done = sem("hh_done")
        hT_done = sem("hT_done")
        d_ready = sem("d_ready")
        acc_done = sem("acc_done")
        out_done = sem("out_done")
        y_copied = sem("y_copied")
        op_ready = sem("op_ready")
        x_used = sem("x_used")
        x1_done = sem("x1_done")
        x1T_ready = sem("x1T_ready")
        x1T_done = sem("x1T_done")
        q_ready = sem("q_ready")
        q_done = sem("q_done")
        negm_done = sem("negm_done")
        bias_done = sem("bias_done")
        s_ready = sem("s_ready")
        s_added = sem("s_added")
        s_max = sem("s_max")
        s_exp = sem("s_exp")
        pt_ready = sem("pt_ready")
        pt_done = sem("pt_done")
        ao_ready = sem("ao_ready")
        ao_normed = sem("ao_normed")
        aoT_ready = sem("aoT_ready")
        aoT_done = sem("aoT_done")
        wo_ready = sem("wo_ready")
        wo_used = sem("wo_used")
        x2_done = sem("x2_done")
        x2T_ready = sem("x2T_ready")
        x2T_high = sem("x2T_high")
        x2T_done = sem("x2T_done")
        lg_ready = sem("lg_ready")
        lg_done = sem("lg_done")
        lg_exp = sem("lg_exp")
        p_done = sem("p_done")
        pT3_ready = sem("pT3_ready")
        pT3_done = sem("pT3_done")

        block = ctx.enter_context(nc.Block())

        NW = 16
        x_g = a["x"].rearrange("(g b) t d -> g t b d", b=GB)
        ctx_g = a["ctx"].rearrange("(g b) t d -> g t b d", b=GB)
        out_g = out.rearrange("(g b) t d -> g t b d", b=GB)
        mask_g = a["mask"].rearrange("(g b) t -> g b t", b=GB)

        def fold(w):
            return w.rearrange("(c k) n -> k c n", k=P)

        @block.sync
        def _(sp):
            def load_x(i):
                sp.dma_start(x_raw[:, :, :], x_g[i]).then_inc(x_in, 16)

            def load_ctx(i):
                sp.dma_start(ctx_raw, ctx_g[i]).then_inc(ctx_in, 16)

            def load_mask(i):
                sp.dma_start(masks[:, :, :], mask_g[i].unsqueeze(0).to_broadcast([P, GB, P])).then_inc(mask_in, 16)

            def split_expert(f, gate, up, down):
                for q in range(6):
                    halves = (gate[:, q, :], up[:, q, :]) if q < DC else (down[:, q - DC, 0:NI], down[:, q - DC, NI:])
                    if q or not isinstance(f, int):
                        sp.wait_ge(wsplit_done, 6 * f + q)
                    for m, src in enumerate(halves):
                        sp.dma_start(split_in[q % 2][:, m * NI:(m + 1) * NI], src).then_inc(wsplit_in[q % 2], 16)
                sp.wait_ge(wsplit_done, 6 * f + 5)
                sp.dma_start(gu_parts[f], w_gu[:, :, :, :].bitcast(F32)).then_inc(gu_out, 16)
                sp.wait_ge(wsplit_done, 6 * f + 7)
                sp.dma_start(down_parts[f], w_down[:, :, :, :].bitcast(F32)).then_inc(down_out, 16)

            def load_expert(f, e):
                sp.wait_ge(up_ready, 2 * f + 1)
                sp.dma_start(w_gu[:, :, :, :].bitcast(F32), gu_parts[e]).then_inc(gu_in, 16)
                sp.wait_ge(d_ready, 4 * f + 1)
                sp.dma_start(w_down[:, :, :, :].bitcast(F32), down_parts[e]).then_inc(down_in, 16)

            def load_stage(e, half, v_e):
                for s in range(3):
                    sp.dma_start(stage[s * NJ:(s + 1) * NJ, half, :, :],
                                 bc_dram.rearrange("(v e n) s t -> e s n v t", v=2, n=NJ)[v_e, s]).then_inc(stage_in, 16)

            def group(i, ffn):
                f0 = (i - 1) * NE
                if ffn:
                    load_expert(f0, 0)
                sp.wait_ge(split_done, i + 1)
                sp.dma_start(bc_dram[:, :, :], bc_parts[:, :, :]).then_inc(bc_out, 16)
                sp.wait_ge(bc_out, 16 * (i + 1))
                load_stage(i, 0, 0)
                with sp.Fori(0, E // 2) as ee:
                    for h in range(2):
                        e = ee * 2 + h
                        if ffn:
                            load_expert(f0 + 1 + e, e + 1)
                        else:
                            w = a["gate_up"][e].rearrange("(c k) n -> k c n", k=P)
                            split_expert(e + 1, w[:, :, 0:NI], w[:, :, NI:],
                                         a["down"][e].rearrange("(c k) n -> k c n", k=P))
                        sp.wait_ge(c_ready, i * (NS + 1) + e * NJ + 1)
                        load_stage(i, 1 - h, (e + 1) % E)
                sp.wait_ge(scan_done, 4 * NS * (i + 1) + 5)
                load_ctx((i + 1) % GROUPS)
                sp.wait_ge(ub_done, 3 * NS * (i + 1))
                sp.wait_ge(ub3_done, NS * (i + 1) + 2)
                for c in range(KV):
                    for j in range(HPG):
                        sp.dma_start(kT[j * DH:(j + 1) * DH, c, :], k_one[c * DH:(c + 1) * DH, :]).then_inc(k_spread, 16)
                sp.wait_ge(x_used, (i + 1) * GB)
                load_x((i + 1) % GROUPS)
                load_mask((i + 1) % GROUPS)

            load_x(0)
            for dst, src in (
                (ident[:, :], a["ident"][:, :]),
                (chan[:, :, :], a["chan"][:, :, :]),
                (w_k[:, :, :], fold(a["Wk"])), (w_v[:, :, :], fold(a["Wv"])),
                (w_xproj[:, :, :], fold(a["xprojT"])), (w_dt[:, :], a["dtprojT"][:, :]),
                (a_neg[:, :, :], a["A_log"].rearrange("(c p) n -> p c n", p=P)),
                (pickb32[:, :], a["picks"][:, :]), (pickp32[:, :], a["pickp"][:, :]),
                (w_out[:, :, :], fold(a["outT"])), (w_q[:, :, :], fold(a["Wq"])),
                (w_o[:, :, :], fold(a["Wo"])), (router32[:, :, :], fold(a["router"])),
                (alibi[:, :, :, :], a["alibi"][:, :, :, :]), (tri[:, :, :], a["tri"][:, :, :]),
            ):
                sp.dma_start(dst, src).then_inc(weights_in, 16)
            load_ctx(0)
            load_mask(0)
            split_expert(0, fold(a["sgate"]), fold(a["sup"]), fold(a["sdown"]))
            group(0, False)
            sp.wait_ge(gu_out, 16 * NE)
            sp.wait_ge(down_out, 16 * NE)
            with sp.Fori(1, GROUPS) as i:
                group(i, True)
            f0 = (GROUPS - 1) * NE
            with sp.Fori(0, NE) as e:
                load_expert(f0 + e, e)
            sp.wait_ge(x_in, 16 * (GROUPS + 1))
            sp.wait_ge(ctx_in, 16 * (GROUPS + 1))
            sp.wait_ge(mask_in, 16 * (GROUPS + 1))

        @block.tensor
        def _(pe):
            mm = nc.tensor.matmul

            def k_sum(dst, lhs, rhs, n=DC):
                for k in range(n):
                    r = mm(dst, lhs(k), rhs(k), start=(k == 0), stop=(k == n - 1))
                return r

            def k_sum_halves(dst, lhs, rhs, n):
                for k in range(n):
                    mm(dst, lhs(0, k), rhs(0, k), start=(k == 0), stop=False)
                    mm(dst, lhs(0, k), rhs(1, k), start=False, stop=False)
                    r = mm(dst, lhs(1, k), rhs(0, k), start=False, stop=(k == n - 1))
                return r

            def turn(src, banks, ready, before=None):
                for c in range(DC):
                    if before:
                        before(c)
                    for b in range(GB):
                        r = nc.tensor.transpose(bank(banks[c])[:, b * P:(b + 1) * P],
                                                src[:, b, c * P:(c + 1) * P], ident[:, :])
                    r.then_inc(ready, 1)

            def ffn_gate(f, e, c):
                if c == 0:
                    pe.wait_ge(acc_done, 4 * f + 1)
                    mm(bank(7), pick_p[:, bass.ds(e, 1)].to_broadcast([25, P]), p_T3[:, :],
                       start=True, stop=True).then_inc(pb_ready, 1)
                    pe.wait_ge(gu_in, 16 * (f + 1))
                else:
                    pe.wait_ge(pg_done, 2 * f + 2)
                k_sum_halves(bank(6), lambda h, k: w_gu[:, h, k, c * P:(c + 1) * P],
                             lambda h, k: x2T[:, h, k, :], DC).then_inc(g_ready, 1)

            def ffn_up(f, c):
                if c == 0:
                    pe.wait_ge(pb_copied, f + 1)
                else:
                    pe.wait_ge(h_done, 2 * f + 1)
                k_sum_halves(bank(7), lambda h, k: w_gu[:, h, k, NI + c * P:NI + (c + 1) * P],
                             lambda h, k: x2T[:, h, k, :], DC).then_inc(up_ready, 1)

            def ffn_down(f, b):
                if b == 0:
                    pe.wait_ge(hT_done, 2 * f + 3)
                    pe.wait_ge(down_in, 16 * (f + 1))
                if b >= 2:
                    pe.wait_ge(acc_done, 4 * f + b)
                k_sum_halves(bank(6 + b % 2), lambda h, k: hT[:, h, k, b * P:(b + 1) * P],
                             lambda h, k: w_down[:, h, k, :], 2).then_inc(d_ready, 1)

            def ffn_piece(f, e, j):
                if j in (0, 2):
                    ffn_gate(f, e, j // 2)
                elif j in (1, 3):
                    ffn_up(f, j // 2)
                else:
                    ffn_down(f, j - 4)

            def spread_b(n2, j, half):
                mm(bank(4 + n2), pick_bc[:, j:j + 1].to_broadcast([3 * NJ, P]), stage[:, half, 0, :],
                   start=True, stop=True).then_inc(b_ready, 1)

            def spread_c(n2, j, half):
                mm(bank(5 - n2), pick_bc[:, j:j + 1].to_broadcast([3 * NJ, P]), stage[:, half, 1, :],
                   start=True, stop=True).then_inc(c_ready, 1)

            def context(g, first):
                if not first:
                    pe.wait_ge(s_added, HPG * GB * g)
                pe.wait_ge(ctx_in, 16 * (g + 1))
                turn(ctx_raw, (0, 1, 2, 3), cT_ready)
                pe.wait_ge(cT_done, DC * (g + 1))
                k_sum(bank(4), lambda k: w_k[:, k, :], lambda k: ctxT[:, k, :]).then_inc(k_ready, 1)
                for b in range(GB):
                    r = k_sum(bank(5)[:, b * P:(b + 1) * P], lambda k: ctxT[:, k, b * P:(b + 1) * P],
                              lambda k: w_v[:, k, :])
                r.then_inc(v_ready, 1)

            def turn_x(g):
                pe.wait_ge(xhat_done, GB * (g + 1))
                turn(xhat, (0, 1, 2, 3), xhT_ready)
                pe.wait_ge(k_done, g + 1)
                pe.wait_ge(v_done, g + 1)
                turn(x_raw, (4, 5, 4, 5), xT_ready,
                     lambda c: pe.wait_ge(xT_done, DC * g + c - 1) if c >= 2 else None)

            def group(i, ffn):
                f0 = (i - 1) * NE
                if ffn:
                    pe.wait_ge(p_done, i)
                    for b in range(GB):
                        r = nc.tensor.transpose(bank(7)[0:3 * E, b * P:(b + 1) * P], p3f[:, b, :], ident[:, :])
                    r.then_inc(pT3_ready, 1)
                pe.wait_ge(xn_done, DC * (i + 1))
                k_sum(bank(1), lambda k: w_xproj[:, k, P:], lambda k: xnT[:, k, :]).then_inc(proj_ready, 1)
                k_sum(bank(0), lambda k: w_xproj[:, k, 0:P], lambda k: xnT[:, k, :]).then_inc(proj_ready, 1)
                if ffn:
                    pe.wait_ge(pT3_done, i)
                    ffn_piece(f0, 0, 0)
                pe.wait_ge(delta_done, i + 1)
                pe.wait_ge(xT_done, DC * (i + 1))
                for c, k in enumerate((2, 3, 4, 5)):
                    mm(bank(k), w_dt[:, c * P:(c + 1) * P], delta, start=True, stop=True).then_inc(z_ready, 1)
                if ffn:
                    ffn_piece(f0, 0, 1)
                pe.wait_ge(split_done, i + 1)
                pe.wait_ge(z_abs, DC * (i + 1))
                pe.wait_ge(z_relu, DC * (i + 1))
                for c in range(DC):
                    r = mm(bank(c), d_diag[:, c, :], xT[:, c, :], start=True, stop=False, skip_group_check=True)
                r.then_inc(y_init, 1)
                pe.wait_ge(stage_in, 48 * (9 * i + 1))
                spread_b(0, 0, 0)
                spread_c(0, 0, 0)
                if ffn:
                    for j in range(2, 8):
                        ffn_piece(f0, 0, j)
                with pe.Fori(0, E // 2) as ee:
                    for h in range(2):
                        e = ee * 2 + h
                        for j in range(NJ):
                            n = e * NJ + j
                            nn = i * NS + n
                            if ffn:
                                ffn_piece(f0 + 1 + e, e + 1, j)
                            half = h
                            if j == NJ - 1:
                                half = 1 - h
                                pe.wait_ge(stage_in, 48 * (9 * i + 2 + e))
                            pe.wait_ge(c_copied, nn + 1)
                            spread_b((j + 1) % 2, (j + 1) % NJ, half)
                            for c in range(DC):
                                if c == 2:
                                    pe.wait_ge(ub_done, 3 * nn + 3)
                                    spread_c((j + 1) % 2, (j + 1) % NJ, half)
                                pe.wait_ge(hc_done, 4 * nn + c + 6)
                                mm(bank(c), ident[:, :], hC[:, c, :], start=False, stop=False,
                                   skip_group_check=True).then_inc(y_added, 1)
                if ffn:
                    pe.wait_ge(acc_done, 4 * (f0 + NE) + 1)
                pe.wait_ge(y_copied, DC * (i + 1))
                for b in range(GB):
                    k_sum(bank(4 + b), lambda k: yT[:, k, b * P:(b + 1) * P],
                          lambda k: w_out[:, k, :]).then_inc(op_ready, 1)
                pe.wait_ge(x1_done, GB * (i + 1))
                turn(x1, (0, 1, 2, 3), x1T_ready)
                pe.wait_ge(x1T_done, DC * (i + 1))
                for c in range(DC):
                    k_sum(bank(4 + c), lambda k: w_q[:, k, c * P:(c + 1) * P],
                          lambda k: x1T[:, k, :]).then_inc(q_ready, 1)

                def scores(b):
                    bb = i * GB + b
                    if b == 0:
                        pe.wait_ge(k_spread, 16 * HEADS * (i + 1))
                        pe.wait_ge(q_done, DC * (i + 1))
                    else:
                        pe.wait_ge(s_added, HPG * bb)
                    for c in range(KV):
                        for j in range(HPG):
                            r = mm(bank(j)[:, c * P:(c + 1) * P], qT[j * DH:(j + 1) * DH, c, b * P:(b + 1) * P],
                                   kT[j * DH:(j + 1) * DH, c, b * P:(b + 1) * P], start=True, stop=True)
                    r.then_inc(s_ready, 1)

                def turn_ao(b):
                    pe.wait_ge(ao_normed, i * GB + b + 1)
                    for c in range(KV):
                        r = nc.tensor.transpose(bank(6)[:, c * P:(c + 1) * P], ao_q[:, c * P:(c + 1) * P], ident[:, :])
                    r.then_inc(aoT_ready, 1)

                def project_ao(b):
                    pe.wait_ge(aoT_done, i * GB + b + 1)
                    k_sum(bank(7), lambda k: aoT[:, k, b * P:(b + 1) * P], lambda k: w_o[:, k, :]).then_inc(wo_ready, 1)

                scores(0)
                for b in range(GB):
                    bb = i * GB + b
                    if b + 1 < GB:
                        scores(b + 1)
                    if b >= 1:
                        turn_ao(b - 1)
                    for c in range(KV):
                        pe.wait_ge(s_exp, HEADS * bb + HPG * (c + 1))
                        if c or b or ffn:
                            pe.wait_ge(pt_done, KV * bb + c)
                        for j in range(HPG):
                            r = nc.tensor.transpose(bank(4 + c % 2)[:, j * P:(j + 1) * P], probs[b % 2][:, j, c, :], ident[:, :])
                        r.then_inc(pt_ready, 1)
                    if b >= 1:
                        project_ao(b - 1)
                    for c in range(KV):
                        pe.wait_ge(pt_done, KV * bb + c + 2)
                        if c == 2:
                            pe.wait_ge(wo_used, bb + 1)
                        for j in range(HPG):
                            o = ((c % 2) * HPG + j) * (DH + 1)
                            r = mm(bank(6 + c // 2)[:, o:o + DH + 1], pT[:, c, j * P:(j + 1) * P], v_sb[:, b, c, :],
                                   start=True, stop=True)
                    r.then_inc(ao_ready, 1)
                turn_ao(GB - 1)
                project_ao(GB - 1)
                context(i + 1, False)
                pe.wait_ge(x2_done, GB * (i + 1))
                turn(acc, (0, 1, 2, 3), x2T_ready)
                pe.wait_ge(x2T_done, DC * (i + 1))
                for b in range(GB):
                    r = k_sum(bank(6)[:, b * E:(b + 1) * E], lambda m: x2T[:, m % 2, m // 4, b * P:(b + 1) * P],
                              lambda m: w_router[:, m // 2 % 2, m // 4, :], 4 * DC)
                r.then_inc(lg_ready, 1)
                turn_x(i + 1)

            pe.wait_ge(weights_in, 16 * (NW - 1))
            pe.wait_ge(consts, 4)
            context(0, True)
            turn_x(0)
            group(0, False)
            with pe.Fori(1, GROUPS) as i:
                group(i, True)
            pe.wait_ge(p_done, GROUPS)
            for b in range(GB):
                r = nc.tensor.transpose(bank(7)[0:3 * E, b * P:(b + 1) * P], p3f[:, b, :], ident[:, :])
            r.then_inc(pT3_ready, 1)
            pe.wait_ge(pT3_done, GROUPS)
            with pe.Fori(0, NE) as e:
                for j in range(8):
                    ffn_piece((GROUPS - 1) * NE + e, e, j)

        @block.scalar
        def _(act):
            act_fn = nc.scalar.activation

            def ffn_copy(f):
                act.wait_ge(pb_ready, f + 1)
                act.wait_ge(pg_done, 2 * f + 1)
                act_fn(pbc[:, :], bank(7), ACT.Copy).then_inc(pb_copied, 1)

            def ffn_tanh(f, c):
                act.wait_ge(pg_done, 2 * f + c + 2)
                act.wait_ge(hT_done, 2 * f + c + 1)
                act_fn(th[:, :], pG[:, :], ACT.Tanh, scale=0.5).then_inc(th_done, 1)

            def exps(i, n, c):
                nn = i * NS + n
                act.wait_ge(scan_done, 4 * nn + c + 2)
                act_fn(dA[:, c, :, 1:P], dtT[:, c, :].rearrange("p (b t) -> p b t", b=GB)[:, :, 1:P], ACT.Exp,
                       scale=a_neg[:, c, bass.ds(n, 1)]).then_inc(da_ready, 1)

            def context(g):
                for c in range(DC):
                    act.wait_ge(cT_ready, DC * g + c + 1)
                    act_fn(ctxT[:, c, :], bank(c), ACT.Copy).then_inc(cT_done, 1)
                act.wait_ge(k_ready, g + 1)
                act_fn(k_one[:, :], bank(4), ACT.Copy).then_inc(k_done, 1)

            def normed_x(g):
                for c in range(DC):
                    act.wait_ge(xhT_ready, DC * g + c + 1)
                    act_fn(xnT[:, c, :], bank(c), ACT.Identity, scale=chan[:, 0, c:c + 1],
                           bias=chan[:, 1, c:c + 1]).then_inc(xn_done, 1)

            def group(i, ffn):
                f0 = (i - 1) * NE
                if ffn:
                    act.wait_ge(pT3_ready, i)
                    act_fn(p_T3[0:3 * E, :], bank(7)[0:3 * E, :], ACT.Copy).then_inc(pT3_done, 1)
                act.wait_ge(proj_ready, 2 * i + 2)
                act_fn(delta, bank(0), ACT.Copy).then_inc(delta_done, 1)
                if ffn:
                    ffn_copy(f0)
                for c, k in enumerate((2, 3, 4, 5)):
                    act.wait_ge(z_ready, DC * i + c + 1)
                    act_fn(dtT[:, c, :], bank(k), ACT.Abs, bias=chan[:, 2, c:c + 1]).then_inc(z_abs, 1)
                if ffn:
                    ffn_tanh(f0, 0)
                act.wait_ge(z_abs, DC * (i + 1))
                for c in range(DC):
                    act_fn(dtT[:, c, :], dtT[:, c, :], ACT.Exp, scale=-1.0).then_inc(act_link, 1)
                act.wait_ge(act_link, DC * (i + 1))
                for c in range(DC):
                    act_fn(dtT[:, c, :], dtT[:, c, :], ACT.Ln, bias=1.0).then_inc(z_log, 1)
                if ffn:
                    ffn_tanh(f0, 1)
                act.wait_ge(u_done, i + 1)
                with act.Fori(0, E // 2) as ee:
                    for h in range(2):
                        e = ee * 2 + h
                        f = f0 + 1 + e
                        for j in range(NJ):
                            n = e * NJ + j
                            nn = i * NS + n
                            act.wait_ge(b_ready, i * (NS + 1) + n + 1)
                            act.wait_ge(ub3_done, nn + 1)
                            act_fn(bc_sb[:, 0, j % 2, :], bank(4 + j % 2), ACT.Copy).then_inc(b_copied, 1)
                            exps(i, n, 0)
                            exps(i, n, 1)
                            act.wait_ge(c_ready, i * (NS + 1) + n + 1)
                            act.wait_ge(hc_done, 4 * nn + 1)
                            act_fn(bc_sb[:, 1, j % 2, :], bank(5 - j % 2), ACT.Copy).then_inc(c_copied, 1)
                            if ffn and j in (1, 3):
                                ffn_tanh(f, j // 2)
                            exps(i, n, 2)
                            exps(i, n, 3)
                            if ffn and j == 0:
                                ffn_copy(f)
                act.wait_ge(y_added, 4 * NS * (i + 1) + 4)
                for c in range(2):
                    act_fn(yT[:, c, :], bank(c), ACT.Copy).then_inc(y_copied, 1)
                for c in range(DC):
                    act.wait_ge(x1T_ready, DC * i + c + 1)
                    act_fn(x1T[:, c, :], bank(c), ACT.Copy).then_inc(x1T_done, 1)
                for c in range(DC):
                    act.wait_ge(q_ready, DC * i + c + 1)
                    act_fn(qT[:, c, :], bank(4 + c), ACT.Copy, scale=float(1.0 / np.sqrt(DH))).then_inc(q_done, 1)

                def softmax_exp(b):
                    act.wait_ge(s_max, i * GB + b + 1)
                    for c in range(KV):
                        for j in range(HPG):
                            r = j * KV + c
                            act_fn(probs[b % 2][:, j, c, :], probs[b % 2][:, j, c, :], ACT.Exp,
                                   bias=mx[:, b % 2, r:r + 1]).then_inc(s_exp, 1)

                def turned_probs(b):
                    bb = i * GB + b
                    for c in range(KV):
                        act.wait_ge(pt_ready, KV * bb + c + 1)
                        act.wait_ge(ao_ready, bb + 1)
                        act_fn(pT[:, c, :], bank(4 + c % 2), ACT.Copy).then_inc(pt_done, 1)

                def turned_ao(b):
                    act.wait_ge(aoT_ready, i * GB + b + 1)
                    act_fn(aoT[:, :, b * P:(b + 1) * P], bank(6).rearrange("p (c q) -> p c q", c=KV),
                           ACT.Copy).then_inc(aoT_done, 1)

                softmax_exp(0)
                turned_probs(0)
                for b in range(1, GB):
                    softmax_exp(b)
                    turned_ao(b - 1)
                    turned_probs(b)
                turned_ao(GB - 1)
                context(i + 1)
                for c in range(DC):
                    act.wait_ge(x2T_ready, DC * i + c + 1)
                    act_fn(x2T[:, 0, c, :], bank(c), ACT.Copy).then_inc(x2T_high, 1)
                act.wait_ge(lg_done, i + 1)
                act_fn(el[:, :, :], lg[:, :, :], ACT.Exp, scale=-1.0).then_inc(lg_exp, 1)
                normed_x(i + 1)

            act.wait_ge(weights_in, 16 * (NW - 1))
            act_fn(a_neg[:, :, :], a_neg[:, :, :], ACT.Exp).then_inc(a_exp, 1)
            act.wait_ge(consts, 4)
            context(0)
            normed_x(0)
            group(0, False)
            with act.Fori(1, GROUPS) as i:
                group(i, True)
            act.wait_ge(pT3_ready, GROUPS)
            act_fn(p_T3[0:3 * E, :], bank(7)[0:3 * E, :], ACT.Copy).then_inc(pT3_done, 1)
            with act.Fori(0, NE) as e:
                f = (GROUPS - 1) * NE + e
                ffn_copy(f)
                ffn_tanh(f, 0)
                ffn_tanh(f, 1)

        @block.vector
        def _(dve):
            v = nc.vector

            class Link:

                def __init__(self, s, per):
                    self.sem, self.per, self.base, self.n = s, per, 0, 0

                def start(self, turn):
                    self.base, self.n = turn * self.per, 0

                def __call__(self, ins):
                    ins.then_inc(self.sem, 1)
                    self.n += 1
                    dve.wait_ge(self.sem, self.base + self.n)

                def end(self):
                    assert self.n == self.per, self.n

            link = Link(dve_link, 26)
            ln = Link(ln_link, 17)

            def norm(number, src, dst, done):
                ln.start(number)
                for b in range(GB):
                    last = v.bn_stats(stats[:, b, :], src[:, b, :])
                ln(last)
                v.memset(nt[:, :], 0.0)
                for b in range(GB):
                    last = v.bn_aggr(mv[:, b, :], stats[:, b, :])
                ln(last)
                ln(v.tensor_scalar(mv[:, :, 1], mv[:, :, 1], EPS, None, ALU.add))
                ln(v.tensor_scalar(rseed[:, :], mv[:, :, 1].bitcast(I32), 1, None, ALU.logical_shift_right))
                ln(v.tensor_scalar(rstd[:, :].bitcast(I32), rseed[:, :], -1, RSQRT_SEED, ALU.mult, ALU.add))
                for _ in range(4):
                    ln(v.tensor_tensor(nt[:, :], rstd[:, :], rstd[:, :], ALU.mult))
                    ln(v.scalar_tensor_tensor(nt[:, :], nt[:, :], -0.5, mv[:, :, 1], ALU.mult, ALU.mult))
                    ln(v.scalar_tensor_tensor(rstd[:, :], nt[:, :], 1.5, rstd[:, :], ALU.add, ALU.mult))
                ln.end()
                for b in range(GB):
                    v.tensor_scalar(dst[:, b, :], src[:, b, :], mv[:, b, 0:1], rstd[:, b:b + 1],
                                    ALU.subtract, ALU.mult).then_inc(done, 1)

            def ffn_pg(f, c):
                dve.wait_ge(g_ready, 2 * f + c + 1)
                dve.wait_ge(pb_copied, f + 1)
                v.tensor_tensor(pG[:, :], bank(6), pbc[:, :], ALU.mult).then_inc(pg_done, 1)

            def ffn_h(f, c):
                dve.wait_ge(th_done, 2 * f + c + 1)
                v.scalar_tensor_tensor(th[:, :], th[:, :], 1.0, pG[:, :], ALU.add, ALU.mult).then_inc(s_done, 1)
                dve.wait_ge(s_done, 2 * f + c + 1)
                dve.wait_ge(up_ready, 2 * f + c + 2)
                v.scalar_tensor_tensor(th[:, :], th[:, :], 0.5, bank(7), ALU.mult, ALU.mult).then_inc(h_done, 1)
                dve.wait_ge(h_done, 2 * f + c + 1)
                v.tensor_copy(hT[:, 0, c, :], th[:, :]).then_inc(hh_done, 1)
                dve.wait_ge(hh_done, 2 * f + c + 1)
                v.tensor_tensor(hT[:, 1, c, :], th[:, :], hT[:, 0, c, :].bitcast(F32),
                                ALU.subtract).then_inc(hT_done, 1)

            def ffn_acc(f, e, b):
                dve.wait_ge(d_ready, 4 * f + b + 2)
                v.scalar_tensor_tensor(acc[:, b, :], bank(6 + b % 2), p_t[:, b, bass.ds(e, 1)], acc[:, b, :],
                                       ALU.mult, ALU.add).then_inc(acc_done, 1)

            def ffn_piece(f, e, j):
                if j in (0, 2):
                    ffn_pg(f, j // 2)
                elif j in (1, 3):
                    ffn_h(f, j // 2)
                else:
                    ffn_acc(f, e, j - 4)

            def split_tile(f, q):
                dst = w_gu[:, :, q, :] if q < DC else w_down[:, :, q - DC, :]
                src = split_in[q % 2][:, :]
                dve.wait_ge(wsplit_in[q % 2], 32 * (3 * f + q // 2 + 1))
                if q in (0, DC) and not (isinstance(f, int) and f == 0):
                    dve.wait_ge(down_out if q else gu_out, 16 * f)
                v.tensor_copy(dst[:, 0, :], src).then_inc(wsplit_high, 1)
                dve.wait_ge(wsplit_high, 6 * f + q + 1)
                v.tensor_tensor(dst[:, 1, :], src, dst[:, 0, :].bitcast(F32), ALU.subtract).then_inc(wsplit_done, 1)

            def values(g):
                dve.wait_ge(v_ready, g + 1)
                v.tensor_copy(v_sb[:, :, :, 0:DH], bank(5).rearrange("p (b c d) -> p b c d", b=GB, c=KV)).then_inc(v_done, 1)

            def normed_x(number, g):
                dve.wait_ge(x_in, 16 * (g + 1))
                norm(number, x_raw, xhat, xhat_done)

            def turned_x(g):
                for c in range(DC):
                    dve.wait_ge(xT_ready, DC * g + c + 1)
                    v.tensor_copy(xT[:, c, :], bank(4 + c % 2)).then_inc(xT_done, 1)

            def group(i, ffn):
                f0 = (i - 1) * NE
                n0 = 4 * i if ffn else 1
                link.start(i)
                v.memset(dA[:, :, :, 0:1], 0.0)
                dve.wait_ge(proj_ready, 2 * i + 1)
                link(v.tensor_copy(bc_parts[:, 0, :], bank(1)))
                link(v.tensor_tensor(resid, bank(1), bc_parts[:, 0, :], ALU.subtract))
                link(v.tensor_copy(bc_parts[:, 1, :], resid))
                v.tensor_tensor(bc_parts[:, 2, :], resid, bc_parts[:, 1, :], ALU.subtract).then_inc(split_done, 1)
                if ffn:
                    ffn_piece(f0, E, 0)
                for c, k in enumerate((2, 3, 4, 5)):
                    dve.wait_ge(z_abs, DC * i + c + 1)
                    v.tensor_scalar(uT[:, c, :], bank(k), chan[:, 2, c:c + 1], 0.0, ALU.add,
                                    ALU.max).then_inc(z_relu, 1)
                if ffn:
                    ffn_piece(f0, E, 1)
                for c in range(DC):
                    dve.wait_ge(z_log, DC * i + c + 1)
                    dve.wait_ge(z_relu, DC * i + c + 1)
                    link(v.tensor_tensor(dtT[:, c, :], dtT[:, c, :], uT[:, c, :], ALU.add))
                    last = v.tensor_tensor(uT[:, c, :], dtT[:, c, :], xnT[:, c, :], ALU.mult)
                last.then_inc(u_done, 1)
                dve.wait_ge(u_done, i + 1)
                dve.wait_ge(y_init, i + 1)
                if ffn:
                    for j in range(2, 8):
                        ffn_piece(f0, E, j)
                else:
                    v.memset(nt[:, :], 0.0)
                with dve.Fori(0, E // 2) as ee:
                    for h in range(2):
                        e = ee * 2 + h
                        for j in range(NJ):
                            nn = i * NS + e * NJ + j
                            dve.wait_ge(b_copied, nn + 1)
                            for c in range(3):
                                dve.wait_ge(scan_done, 4 * nn + c + 2)
                                v.tensor_tensor(uB[:, c, :], uT[:, c, :], bank(4 + j % 2), ALU.mult).then_inc(ub_done, 1)
                            for c in range(DC):
                                if c == 3:
                                    dve.wait_ge(ub3_done, nn + 3)
                                else:
                                    dve.wait_ge(ub_done, 3 * nn + c + 1)
                                dve.wait_ge(da_ready, 4 * nn + c + 1)
                                dve.wait_ge(hc_done, 4 * nn + c + 2)
                                v.tensor_tensor_scan(hs[:, c, :], dA[:, c, :, :].rearrange("p b t -> p (b t)"),
                                                     uB[:, c, :] if c < 3 else ub3(j % 2),
                                                     0.0, ALU.mult, ALU.add).then_inc(scan_done, 1)
                            if ffn:
                                ffn_piece(f0 + 1 + e, e, j)
                            elif j < 6:
                                split_tile(1 + e, j)
                v.memset(nt[:, :], 0.0)
                dve.wait_ge(y_added, 4 * NS * (i + 1) + 4)
                for c in (2, 3):
                    v.tensor_copy(yT[:, c, :], bank(c)).then_inc(y_copied, 1)
                dve.wait_ge(mask_in, 16 * (i + 1))
                v.tensor_scalar(negm[:, :, :], masks[:, :, :], -NEG, NEG, ALU.mult, ALU.add).then_inc(negm_done, 1)
                for b in range(GB):
                    dve.wait_ge(op_ready, GB * i + b + 1)
                    v.tensor_tensor(x1[:, b, :], bank(4 + b), x_raw[:, b, :], ALU.add).then_inc(x_used, 1)
                dve.wait_ge(x_used, GB * (i + 1))
                norm(n0, x1, x1, x1_done)
                if ffn:
                    norm(n0 + 1, acc, acc, out_done)
                    n0 = n0 + 1

                def shift(b):
                    bb = i * GB + b
                    p4 = probs[b % 2]
                    dve.wait_ge(s_ready, bb + 1)
                    dve.wait_ge(bias_done, bb + 1)
                    if b >= 2:
                        dve.wait_ge(pt_ready, KV * (bb - 1))
                    for j in range(HPG):
                        v.tensor_tensor(p4[:, j, :, :], bank(j).rearrange("p (c k) -> p c k", c=KV),
                                        bias[:, j, :, :], ALU.add).then_inc(s_added, 1)
                    dve.wait_ge(s_added, HPG * (bb + 1))
                    link(v.tensor_reduce(rs[:, :], p4.rearrange("p j c k -> p (j c) k"), AX.X, ALU.max))
                    v.tensor_scalar(mx[:, b % 2, :], rs[:, :], -1.0, None, ALU.mult).then_inc(s_max, 1)

                def normed_ao(b):
                    dve.wait_ge(ao_ready, i * GB + b + 2)
                    o = ps[:, 6:8, 0:2 * HPG * (DH + 1)].rearrange("p a (h d) -> p a h d", d=DH + 1)
                    r = sums[:, :].rearrange("p (a h) -> p a h", a=2)
                    link(v.reciprocal(r, o[:, :, :, DH]))
                    v.tensor_tensor(ao_q[:, :].rearrange("p (a h d) -> p a h d", a=2, d=DH), o[:, :, :, 0:DH],
                                    r.unsqueeze(3).to_broadcast([P, 2, 2 * HPG, DH]), ALU.mult).then_inc(ao_normed, 1)

                def residual(b):
                    dve.wait_ge(wo_ready, i * GB + b + 1)
                    if ffn:
                        dve.wait_ge(stored, 16 * i)
                    v.tensor_tensor(acc[:, b, :], bank(7), x1[:, b, :], ALU.add).then_inc(wo_used, 1)

                shift(0)
                shift(1)
                normed_ao(0)
                for b in range(1, GB):
                    if b + 1 < GB:
                        shift(b + 1)
                    residual(b - 1)
                    normed_ao(b)
                residual(GB - 1)
                dve.wait_ge(wo_used, GB * (i + 1) + 1)
                norm(n0 + 1, acc, acc, x2_done)
                normed_x(n0 + 2, i + 1)
                values(i + 1)
                for c in range(DC):
                    dve.wait_ge(x2T_high, DC * i + c + 1)
                    v.tensor_tensor(x2T[:, 1, c, :], bank(c), x2T[:, 0, c, :].bitcast(F32),
                                    ALU.subtract).then_inc(x2T_done, 1)
                dve.wait_ge(lg_ready, i + 1)
                v.tensor_copy(lg[:, :, :].rearrange("p b e -> p (b e)"), bank(6)[:, 0:GB * E]).then_inc(lg_done, 1)
                dve.wait_ge(lg_done, i + 1)
                other = lg[:, :, :].unsqueeze(2).to_broadcast([P, GB, E, E])
                own = lg[:, :, :].unsqueeze(3).to_broadcast([P, GB, E, E])
                v.tensor_tensor(gt[:, :, :, :], other, own, ALU.is_gt)
                link(v.tensor_tensor(eq[:, :, :, :], other, own, ALU.is_equal))
                turned_x(i + 1)
                link(v.tensor_tensor(eq[:, :, :, :], eq[:, :, :, :],
                                     tri[:, :, :].unsqueeze(1).to_broadcast([P, GB, E, E]), ALU.mult))
                link(v.tensor_tensor(gt[:, :, :, :], gt[:, :, :, :], eq[:, :, :, :], ALU.add))
                link(v.tensor_reduce(rank[:, :, :].rearrange("p b e -> p (b e)"),
                                     gt[:, :, :, :].rearrange("p b e o -> p (b e) o"), AX.X, ALU.add))
                dve.wait_ge(lg_exp, i + 1)
                link(v.tensor_scalar(el[:, :, :], el[:, :, :], 1.0, None, ALU.add))
                link(v.reciprocal(el[:, :, :], el[:, :, :]))
                link(v.scalar_tensor_tensor(p_t[:, :, 0:E], rank[:, :, :], 2.0, el[:, :, :], ALU.is_lt, ALU.mult))
                link(v.tensor_copy(p3b[:, :, 0:E], p_t[:, :, 0:E]))
                link(v.tensor_tensor(el[:, :, :], p_t[:, :, 0:E], p3b[:, :, 0:E], ALU.subtract))
                link(v.tensor_copy(p3b[:, :, E:2 * E], el[:, :, :]))
                link(v.tensor_tensor(p3b[:, :, 2 * E:], el[:, :, :], p3b[:, :, E:2 * E], ALU.subtract))
                v.tensor_copy(p3f[:, :, :], p3b[:, :, :]).then_inc(p_done, 1)
                link.end()

            for k, free in enumerate((up_ready, d_ready, acc_done, pg_done, hT_done, ao_ready, wo_used, pt_done,
                                      wsplit_done)):
                v.memset(mx[:, 0, k:k + 1], 0.0).then_inc(free, 1)
            v.memset(mx[:, 0, 15:16], 0.0).then_inc(scan_done, 5)
            v.memset(p_t[:, :, :], 1.0)
            v.memset(v_sb[:, :, :, :], 1.0)
            v.memset(p_T3[:, :], 1.0).then_inc(consts, 1)
            dve.wait_ge(weights_in, 16 * (NW - 1))
            v.tensor_copy(pick_bc[:, :], pickb32[:, :])
            v.tensor_copy(pick_p[:, :], pickp32[:, :])
            v.tensor_copy(w_router[:, 0, :, :], router32[:, :, :]).then_inc(consts, 1)
            dve.wait_ge(consts, 2)
            v.tensor_tensor(w_router[:, 1, :, :], router32[:, :, :], w_router[:, 0, :, :].bitcast(F32), ALU.subtract)
            for c in range(DC):
                v.tensor_scalar(d_diag[:, c, :], ident[:, :], chan[:, 3, c:c + 1], None, ALU.mult)
            v.memset(mx[:, 0, 14:15], 0.0).then_inc(consts, 1)
            dve.wait_ge(y_added, 4)
            dve.wait_ge(hc_done, 5)
            dve.wait_ge(a_exp, 1)
            v.tensor_scalar(a_neg[:, :, :], a_neg[:, :, :], -1.0, None, ALU.mult).then_inc(consts, 1)
            dve.wait_ge(consts, 4)
            normed_x(0, 0)
            values(0)
            turned_x(0)
            for q in range(6):
                split_tile(0, q)
            group(0, False)
            with dve.Fori(1, GROUPS) as i:
                group(i, True)
            with dve.Fori(0, E + 1) as e:
                for j in range(8):
                    ffn_piece((GROUPS - 1) * NE + e, (e + E) % NE, j)
            dve.wait_ge(acc_done, 4 * NE * GROUPS + 1)
            norm(4 * GROUPS, acc, acc, out_done)

        @block.gpsimd
        def _(pool):
            g = nc.gpsimd

            def group(i, ffn):
                with pool.Fori(0, E // 2) as ee:
                    for h in range(2):
                        for j in range(NJ):
                            nn = i * NS + (ee * 2 + h) * NJ + j
                            if h == 0 and j == 0:
                                pool.wait_ge(u_done, i + 1)
                            pool.wait_ge(b_copied, nn + 1)
                            pool.wait_ge(scan_done, 4 * nn + 1)
                            g.tensor_tensor(ub3(j % 2), uT[:, 3, :], bc_sb[:, 0, j % 2, :], ALU.mult).then_inc(ub3_done, 1)
                            pool.wait_ge(c_copied, nn + 1)
                            for c in range(DC):
                                pool.wait_ge(scan_done, 4 * nn + c + 6)
                                pool.wait_ge(y_added, 4 * nn + c + 1)
                                g.tensor_tensor(hC[:, c, :], hs[:, c, :], bc_sb[:, 1, j % 2, :],
                                                ALU.mult).then_inc(hc_done, 1)

                def add_bias(b):
                    g.tensor_tensor(bias, alibi[:, :, :, :],
                                    negm[:, b, :].unsqueeze(1).unsqueeze(1).to_broadcast([P, HPG, KV, P]),
                                    ALU.add).then_inc(bias_done, 1)

                pool.wait_ge(negm_done, i + 1)
                add_bias(0)
                if ffn:
                    pool.wait_ge(out_done, GB * i)
                    pool.dma_start(out_g[i - 1], acc[:, :, :]).then_inc(stored, 16)
                for b in range(1, GB):
                    pool.wait_ge(s_added, HPG * (i * GB + b))
                    add_bias(b)

            g.memset(hC[:, :, :], 0.0).then_inc(y_added, 4)
            g.memset(hs[:, :, :], 0.0).then_inc(hc_done, 5)
            g.memset(uB3b[:, :], 0.0).then_inc(ub3_done, 2)
            group(0, False)
            with pool.Fori(1, GROUPS) as i:
                group(i, True)
            pool.wait_ge(out_done, GB * GROUPS)
            pool.dma_start(out_g[GROUPS - 1], acc[:, :, :]).then_inc(stored, 16)
            pool.wait_ge(stored, 16 * GROUPS)


def kernel(**inputs):
    import concourse.bacc as bacc
    from concourse.bass_utils import run_bass_kernel_spmd

    def arr(name):
        return np.asarray(inputs[name])

    picks = np.tile(np.eye(NJ, dtype=np.float32), (3, 1))
    pickp = np.zeros((25, NE), np.float32)
    pickp[24, 0] = 1
    for e in range(E):
        pickp[[e, E + e, 2 * E + e], 1 + e] = 1
    m0 = np.float32(2.0 ** (-8.0 / HEADS))
    slopes = (m0 ** np.arange(1, HEADS + 1, dtype=np.float32)).reshape(KV, HPG).T
    rel = np.arange(P, dtype=np.float32)[None, :] - np.arange(P, dtype=np.float32)[:, None]
    alibi = slopes[None, :, :, None] * rel[:, None, None, :]
    tri = np.broadcast_to(np.tril(np.ones((E, E), np.float32), -1), (P, E, E))
    arrays = {
        "x": arr("x"), "ctx": arr("ctx_2048"), "mask": arr("mask_BxS2_bf1").view(np.uint8),
        "chan": np.stack([arr("L0_attn_norm_w"), arr("L0_attn_norm_b"), arr("L0_attn_dt_proj_b"),
                          arr("L0_attn_D_param")]).reshape(4, DC, P).transpose(2, 0, 1),
        "xprojT": arr("L0_attn_x_proj_w").T, "dtprojT": arr("L0_attn_dt_proj_w").T,
        "A_log": arr("L0_attn_A_log"), "outT": arr("L0_attn_out_proj_w").T,
        "Wq": arr("L0_xattn_Wq"), "Wk": arr("L0_xattn_Wk"), "Wv": arr("L0_xattn_Wv"), "Wo": arr("L0_xattn_Wo"),
        "router": arr("L0_ffn_router_w"), "gate_up": arr("L0_ffn_gate_up_w"), "down": arr("L0_ffn_down_w"),
        "sgate": arr("L0_ffn_shared_gate_w"), "sup": arr("L0_ffn_shared_up_w"), "sdown": arr("L0_ffn_shared_down_w"),
        "ident": np.eye(P, dtype=np.float32), "picks": picks, "pickp": pickp,
        "alibi": alibi.astype(np.float32), "tri": tri,
    }
    nc = bacc.Bacc("TRN2", target_bir_lowering=False, num_devices=1)
    feed, aps = {}, {}
    for name, v in arrays.items():
        v = np.ascontiguousarray(v)
        feed[f"in_{name}"] = v
        aps[name] = nc.dram_tensor(f"in_{name}", v.shape, mybir.dt.from_np(v.dtype), kind="ExternalInput").ap()
    out = nc.dram_tensor("out", (B, P, D), F32, kind="ExternalOutput").ap()
    decoder_layer_kernel(nc, aps, out)
    r = run_bass_kernel_spmd(nc, [feed], core_ids=[0])
    return r.results[0]["out"]
```

```python
from contextlib import ExitStack

import numpy as np

import concourse.bass as bass
from concourse import mybir

ALU = mybir.AluOpType
ACT = mybir.ActivationFunctionType
AX = mybir.AxisListType
F32 = mybir.dt.float32
F32R = mybir.dt.float32r
I32 = mybir.dt.int32
BF16 = mybir.dt.bfloat16
U8 = mybir.dt.uint8

P = 128
B = 32
GB = 4
TG = GB * P
GROUPS = B // GB
D = 512
DC = D // P
NS = 64
NJ = 8
E = 8
NI = 256
NE = E + 1
HEADS = 16
KV = 4
HPG = HEADS // KV
DH = D // HEADS
EPS = 1e-5
RSQRT_SEED = 0x5F3759DF
NEG = float(np.finfo(np.float32).min)


def decoder_layer_kernel(nc, a, out):
    ctx = ExitStack()
    with ctx:
        def sb(name, shape, dt=F32):
            return ctx.enter_context(nc.sbuf_tensor(name, shape, dt))

        def sem(name):
            return ctx.enter_context(nc.semaphore(name))

        w_xproj = sb("w_xproj", [P, DC, P + 2 * NS])
        w_dt = sb("w_dt", [P, D])
        w_out = sb("w_out", [P, DC, D])
        w_q = sb("w_q", [P, DC, D])
        w_k = sb("w_k", [P, DC, P])
        w_v = sb("w_v", [P, DC, P])
        w_o = sb("w_o", [P, DC, D])
        w_router = sb("w_router", [P, DC, 2, E], F32R)
        router32 = sb("router32", [P, DC, E])
        chan = sb("chan", [P, 3, DC])
        a_neg = sb("a_neg", [P, DC, NS])
        d_row = sb("d_row", [P, D])
        ident = sb("ident", [P, P])
        pick_bc = sb("pick_bc", [3 * NJ, NJ], BF16)
        pick_p = sb("pick_p", [25, NE], BF16)
        pickb32 = sb("pickb32", [3 * NJ, NJ])
        pickp32 = sb("pickp32", [25, NE])
        alibi = sb("alibi", [P, HPG, KV, P])
        tri = sb("tri", [P, E, E])
        masks = sb("masks", [P, GB, P], U8)

        x_raw = sb("x_raw", [P, GB, D])
        x1 = sb("x1", [P, GB, D])
        acc = sb("acc", [P, GB, D])
        x2T = sb("x2T", [P, 2, DC, TG], F32R)
        x1T = sb("x1T", [P, DC, TG])
        dtT = sb("dtT", [P, DC, TG])
        uT = sb("uT", [P, DC, TG])
        dA = sb("dA", [P, DC, GB, P])
        hs = sb("hs", [P, DC, TG])
        hC = sb("hC", [P, DC, TG])
        uB = sb("uB", [P, 4, TG])
        uB3b = sb("uB3b", [P, TG])
        bc_sb = sb("bc_sb", [P, 2, 2, TG])
        bc_parts = sb("bc_parts", [P, 3, TG], BF16)
        stage = sb("stage", [3 * NJ, 2, 2, TG], BF16)
        k_one = sb("k_one", [P, TG])
        v_sb = sb("v_sb", [P, GB, KV, DH + 1])
        negm = sb("negm", [P, GB, P])
        w_gu = sb("w_gu", [P, 2, DC, 2 * NI], F32R)
        w_down = sb("w_down", [P, 2, 2, D], F32R)
        hT = sb("hT", [P, 2, 2, TG], F32R)
        pG = sb("pG", [P, TG])
        th = sb("th", [P, TG])
        pbc = sb("pbc", [P, TG])
        p_t = sb("p_t", [P, GB, NE])
        p_T3 = sb("p_T3", [25, TG], BF16)
        stats = sb("stats", [P, GB, 6])
        mv = sb("mv", [P, GB, 2])
        rstd = sb("rstd", [P, GB])
        rseed = sb("rseed", [P, GB], I32)
        nt = sb("nt", [P, GB])
        mx = sb("mx", [P, 2, HEADS])
        rs = sb("rs", [P, HEADS])
        sums = sb("sums", [P, HEADS])
        lg = sb("lg", [P, GB, E])
        el = sb("el", [P, GB, E])
        rank = sb("rank", [P, GB, E])
        p3b = sb("p3b", [P, GB, 3 * E], BF16)
        p3f = sb("p3f", [P, GB, 3 * E])

        xhat = dA[:, :, :, :].rearrange("p c b t -> p c (b t)")
        xD = hC
        xnT = uB
        delta, resid = hs[:, 2, :], hs[:, 3, :]
        lgT = th[0:2 * E, :]
        yT, ctxT, qT = dtT, dtT, dtT
        kT = uT
        aoT = x1T
        ctx_raw = dA[:, :, :, :].rearrange("p c b t -> p c (b t)")
        probs = [t[:, :, :].rearrange("p j (c k) -> p j c k", c=KV) for t in (hs, hC)]
        bias = uB[:, :, :].rearrange("p j (c k) -> p j c k", c=KV)
        pT = bc_sb[:, :, :, :].rearrange("p a b t -> p (a b) t")
        ao_q = uB3b
        split_in = [pG, th]
        gt, eq = (hs[:, m, 0:GB * E * E].rearrange("p (b e o) -> p b e o", b=GB, e=E) for m in range(2))

        def ub3(n2):
            return uB[:, 3, :] if n2 == 0 else uB3b[:, :]

        ps = ctx.enter_context(nc.psum_tensor("ps", [P, 8, 512], F32))

        def bank(k):
            return ps[:, k, :]

        gu_parts = nc.dram_tensor("gu_parts", [NE, P, 2, DC, 2 * NI], F32, kind="Internal").ap()
        down_parts = nc.dram_tensor("down_parts", [NE, P, 2, 2, D], F32, kind="Internal").ap()
        bc_dram = nc.dram_tensor("bc_dram", [2 * NS, 3, TG], BF16, kind="Internal").ap()

        first_in = sem("first_in")
        weights_in = sem("weights_in")
        router_split = sem("router_split")
        a_exp = sem("a_exp")
        wsplit_in = [sem("wsplit_even_in"), sem("wsplit_odd_in")]
        wsplit_done = sem("wsplit_done")
        wsplit_high = sem("wsplit_high")
        gu_out = sem("gu_out")
        down_out = sem("down_out")
        x_in = sem("x_in")
        ctx_in = sem("ctx_in")
        mask_in = sem("mask_in")
        gu_in = sem("gu_in")
        down_in = sem("down_in")
        bc_out = sem("bc_out")
        stage_in = sem("stage_in")
        stored = sem("stored")
        dve_link = sem("dve_link")
        pre_link = sem("pre_link")
        ln_link = sem("ln_link")
        act_link = sem("act_link")
        xhat_done = sem("xhat_done")
        xhT_ready = sem("xhT_ready")
        xn_done = sem("xn_done")
        xd_done = sem("xd_done")
        cT_ready = sem("cT_ready")
        cT_done = sem("cT_done")
        k_ready = sem("k_ready")
        k_done = sem("k_done")
        k_spread = sem("k_spread")
        v_ready = sem("v_ready")
        v_done = sem("v_done")
        proj_ready = sem("proj_ready")
        delta_done = sem("delta_done")
        split_done = sem("split_done")
        z_ready = sem("z_ready")
        z_abs = sem("z_abs")
        z_relu = sem("z_relu")
        z_log = sem("z_log")
        u_done = sem("u_done")
        y_init = sem("y_init")
        b_ready = sem("b_ready")
        c_ready = sem("c_ready")
        b_copied = sem("b_copied")
        c_copied = sem("c_copied")
        ub_done = sem("ub_done")
        ub3_done = sem("ub3_done")
        da_ready = sem("da_ready")
        scan_done = sem("scan_done")
        hc_done = sem("hc_done")
        y_added = sem("y_added")
        g_ready = sem("g_ready")
        up_ready = sem("up_ready")
        pb_ready = sem("pb_ready")
        pb_copied = sem("pb_copied")
        pg_done = sem("pg_done")
        th_done = sem("th_done")
        s_done = sem("s_done")
        h_done = sem("h_done")
        hh_done = sem("hh_done")
        hT_done = sem("hT_done")
        d_ready = sem("d_ready")
        acc_done = sem("acc_done")
        out_done = sem("out_done")
        y_copied = sem("y_copied")
        op_ready = sem("op_ready")
        x_used = sem("x_used")
        x1_done = sem("x1_done")
        x1T_ready = sem("x1T_ready")
        x1T_done = sem("x1T_done")
        q_ready = sem("q_ready")
        q_done = sem("q_done")
        negm_done = sem("negm_done")
        bias_done = sem("bias_done")
        s_ready = sem("s_ready")
        s_added = sem("s_added")
        s_max = sem("s_max")
        s_exp = sem("s_exp")
        pt_ready = sem("pt_ready")
        pt_done = sem("pt_done")
        ao_ready = sem("ao_ready")
        ao_normed = sem("ao_normed")
        aoT_ready = sem("aoT_ready")
        aoT_done = sem("aoT_done")
        wo_ready = sem("wo_ready")
        wo_used = sem("wo_used")
        x2_done = sem("x2_done")
        x2T_ready = sem("x2T_ready")
        x2T_high = sem("x2T_high")
        x2T_done = sem("x2T_done")
        lgT_ready = sem("lgT_ready")
        lgT_done = sem("lgT_done")
        lg_ready = sem("lg_ready")
        lg_done = sem("lg_done")
        lg_exp = sem("lg_exp")
        p_done = sem("p_done")
        pT3_ready = sem("pT3_ready")
        pT3_done = sem("pT3_done")

        block = ctx.enter_context(nc.Block())

        FIRST_LOADS, WEIGHT_LOADS = 8, 8
        x_g = a["x"].rearrange("(g b) t d -> g t b d", b=GB)
        ctx_g = a["ctx"].rearrange("(g b) t d -> g t b d", b=GB)
        out_g = out.rearrange("(g b) t d -> g t b d", b=GB)
        mask_g = a["mask"].rearrange("(g b) t -> g b t", b=GB)

        def fold(w):
            return w.rearrange("(c k) n -> k c n", k=P)

        @block.sync
        def _(sp):
            def load_x(i):
                sp.dma_start(x_raw[:, :, :], x_g[i]).then_inc(x_in, 16)

            def load_ctx(i):
                sp.dma_start(ctx_raw, ctx_g[i]).then_inc(ctx_in, 16)

            def load_mask(i):
                sp.dma_start(masks[:, :, :], mask_g[i].unsqueeze(0).to_broadcast([P, GB, P])).then_inc(mask_in, 16)

            def load_split(f, halves, q):
                gate, up, down = halves
                srcs = (gate[:, q, :], up[:, q, :]) if q < DC else (down[:, q - DC, 0:NI], down[:, q - DC, NI:])
                if q or not isinstance(f, int):
                    sp.wait_ge(wsplit_done, 6 * f + q)
                for m, src in enumerate(srcs):
                    sp.dma_start(split_in[q % 2][:, m * NI:(m + 1) * NI], src).then_inc(wsplit_in[q % 2], 16)

            def store_split(f):
                sp.wait_ge(wsplit_done, 6 * f + 5)
                sp.dma_start(gu_parts[f], w_gu[:, :, :, :].bitcast(F32)).then_inc(gu_out, 16)
                sp.wait_ge(wsplit_done, 6 * f + 7)
                sp.dma_start(down_parts[f], w_down[:, :, :, :].bitcast(F32)).then_inc(down_out, 16)

            def load_expert(f, e):
                sp.wait_ge(up_ready, 2 * f + 1)
                sp.dma_start(w_gu[:, :, :, :].bitcast(F32), gu_parts[e]).then_inc(gu_in, 16)
                sp.wait_ge(d_ready, 4 * f + 1)
                sp.dma_start(w_down[:, :, :, :].bitcast(F32), down_parts[e]).then_inc(down_in, 16)

            def load_stage(e, half, v_e):
                for s in range(3):
                    sp.dma_start(stage[s * NJ:(s + 1) * NJ, half, :, :],
                                 bc_dram.rearrange("(v e n) s t -> e s n v t", v=2, n=NJ)[v_e, s]).then_inc(stage_in, 16)

            def load_bc(g):
                sp.wait_ge(split_done, g + 1)
                sp.dma_start(bc_dram[:, :, :], bc_parts[:, :, :]).then_inc(bc_out, 16)
                sp.wait_ge(bc_out, 16 * (g + 1))
                load_stage(g, 0, 0)

            def group(i, ffn, more=True):
                f0 = (i - 1) * NE
                with sp.Fori(0, E // 2) as ee:
                    for h in range(2):
                        e = ee * 2 + h
                        if ffn:
                            load_expert(f0 + 1 + e, e + 1)
                        else:
                            w = a["gate_up"][e].rearrange("(c k) n -> k c n", k=P)
                            expert = (w[:, :, 0:NI], w[:, :, NI:], a["down"][e].rearrange("(c k) n -> k c n", k=P))
                            for q in range(6):
                                load_split(e + 1, expert, q)
                            store_split(e + 1)
                        sp.wait_ge(c_ready, i * (NS + 1) + e * NJ + 1)
                        load_stage(i, 1 - h, (e + 1) % E)
                sp.wait_ge(scan_done, 4 * NS * (i + 1) + 5)
                load_ctx(i)
                if more:
                    sp.wait_ge(x_used, (i + 1) * GB)
                    load_x(i + 1)
                    load_mask(i + 1)
                sp.wait_ge(k_done, i + 1)
                for c in range(KV):
                    for j in range(HPG):
                        sp.dma_start(kT[j * DH:(j + 1) * DH, c, :], k_one[c * DH:(c + 1) * DH, :]).then_inc(k_spread, 16)
                if not ffn:
                    sp.wait_ge(gu_out, 16 * NE)
                    sp.wait_ge(down_out, 16 * NE)
                load_expert(i * NE, 0)
                if more:
                    load_bc(i + 1)

            shared = (fold(a["sgate"]), fold(a["sup"]), fold(a["sdown"]))
            load_x(0)
            for dst, src in (
                (ident[:, :], a["ident"][:, :]), (chan[:, :, :], a["chan"][:, :, :]),
                (w_xproj[:, :, :], fold(a["xprojT"])), (w_dt[:, :], a["dtprojT"][:, :]),
                (a_neg[:, :, :], a["A_log"].rearrange("(c p) n -> p c n", p=P)),
                (d_row[:, :], a["D"].unsqueeze(0).to_broadcast([P, D])),
                (pickb32[:, :], a["picks"][:, :]), (pickp32[:, :], a["pickp"][:, :]),
            ):
                sp.dma_start(dst, src).then_inc(first_in, 16)
            load_split(0, shared, 0)
            load_split(0, shared, 1)
            load_mask(0)
            for dst, src in (
                (w_k[:, :, :], fold(a["Wk"])), (w_v[:, :, :], fold(a["Wv"])),
                (w_out[:, :, :], fold(a["outT"])), (w_q[:, :, :], fold(a["Wq"])),
                (w_o[:, :, :], fold(a["Wo"])), (router32[:, :, :], fold(a["router"])),
                (alibi[:, :, :, :], a["alibi"][:, :, :, :]), (tri[:, :, :], a["tri"][:, :, :]),
            ):
                sp.dma_start(dst, src).then_inc(weights_in, 16)
            load_split(0, shared, 2)
            load_split(0, shared, 3)
            load_bc(0)
            load_split(0, shared, 4)
            load_split(0, shared, 5)
            store_split(0)
            group(0, False)
            with sp.Fori(1, GROUPS - 1) as i:
                group(i, True)
            group(GROUPS - 1, True, more=False)
            f0 = (GROUPS - 1) * NE
            with sp.Fori(1, NE) as e:
                load_expert(f0 + e, e)
            sp.wait_ge(x_in, 16 * GROUPS)
            sp.wait_ge(ctx_in, 16 * GROUPS)
            sp.wait_ge(mask_in, 16 * GROUPS)

        @block.tensor
        def _(pe):
            mm = nc.tensor.matmul

            def k_sum(dst, lhs, rhs, n=DC):
                for k in range(n):
                    r = mm(dst, lhs(k), rhs(k), start=(k == 0), stop=(k == n - 1))
                return r

            def k_sum_halves(dst, lhs, rhs, n):
                for k in range(n):
                    mm(dst, lhs(0, k), rhs(0, k), start=(k == 0), stop=False)
                    mm(dst, lhs(0, k), rhs(1, k), start=False, stop=False)
                    r = mm(dst, lhs(1, k), rhs(0, k), start=False, stop=(k == n - 1))
                return r

            def turn(src, banks, ready, before=None):
                for c in range(DC):
                    if before:
                        before(c)
                    for b in range(GB):
                        r = nc.tensor.transpose(bank(banks[c])[:, b * P:(b + 1) * P],
                                                src[:, b, c * P:(c + 1) * P], ident[:, :])
                    r.then_inc(ready, 1)

            def ffn_gate(f, e, c):
                if c == 0:
                    pe.wait_ge(acc_done, 4 * f + 1)
                    mm(bank(7), pick_p[:, bass.ds(e, 1)].to_broadcast([25, P]), p_T3[:, :],
                       start=True, stop=True).then_inc(pb_ready, 1)
                    pe.wait_ge(gu_in, 16 * (f + 1))
                else:
                    pe.wait_ge(pg_done, 2 * f + 2)
                k_sum_halves(bank(6), lambda h, k: w_gu[:, h, k, c * P:(c + 1) * P],
                             lambda h, k: x2T[:, h, k, :], DC).then_inc(g_ready, 1)

            def ffn_up(f, c):
                if c == 0:
                    pe.wait_ge(pb_copied, f + 1)
                else:
                    pe.wait_ge(h_done, 2 * f + 1)
                k_sum_halves(bank(7), lambda h, k: w_gu[:, h, k, NI + c * P:NI + (c + 1) * P],
                             lambda h, k: x2T[:, h, k, :], DC).then_inc(up_ready, 1)

            def ffn_down(f, b):
                if b == 0:
                    pe.wait_ge(hT_done, 2 * f + 3)
                    pe.wait_ge(down_in, 16 * (f + 1))
                if b >= 2:
                    pe.wait_ge(acc_done, 4 * f + b)
                k_sum_halves(bank(6 + b % 2), lambda h, k: hT[:, h, k, b * P:(b + 1) * P],
                             lambda h, k: w_down[:, h, k, :], 2).then_inc(d_ready, 1)

            def ffn_piece(f, e, j):
                if j in (0, 2):
                    ffn_gate(f, e, j // 2)
                elif j in (1, 3):
                    ffn_up(f, j // 2)
                else:
                    ffn_down(f, j - 4)

            def spread_b(n2, j, half):
                mm(bank(4 + n2), pick_bc[:, j:j + 1].to_broadcast([3 * NJ, P]), stage[:, half, 0, :],
                   start=True, stop=True).then_inc(b_ready, 1)

            def spread_c(n2, j, half):
                mm(bank(5 - n2), pick_bc[:, j:j + 1].to_broadcast([3 * NJ, P]), stage[:, half, 1, :],
                   start=True, stop=True).then_inc(c_ready, 1)

            def context(g):
                pe.wait_ge(ctx_in, 16 * (g + 1))
                turn(ctx_raw, (0, 1, 2, 3), cT_ready)
                pe.wait_ge(cT_done, DC * (g + 1))
                pe.wait_ge(x_used, GB * (g + 1))
                k_sum(bank(4), lambda k: w_k[:, k, :], lambda k: ctxT[:, k, :]).then_inc(k_ready, 1)
                for b in range(GB):
                    r = k_sum(bank(5)[:, b * P:(b + 1) * P], lambda k: ctxT[:, k, b * P:(b + 1) * P],
                              lambda k: w_v[:, k, :])
                r.then_inc(v_ready, 1)

            def turn_xhat(g):
                pe.wait_ge(xhat_done, GB * (g + 1))
                turn(xhat, (0, 1, 2, 3), xhT_ready)

            def project_x(g):
                pe.wait_ge(xn_done, DC * (g + 1))
                k_sum(bank(1), lambda k: w_xproj[:, k, P:], lambda k: xnT[:, k, :]).then_inc(proj_ready, 1)
                k_sum(bank(0), lambda k: w_xproj[:, k, 0:P], lambda k: xnT[:, k, :]).then_inc(proj_ready, 1)
                pe.wait_ge(delta_done, g + 1)
                for c, k in enumerate((2, 3, 4, 5)):
                    mm(bank(k), w_dt[:, c * P:(c + 1) * P], delta, start=True, stop=True).then_inc(z_ready, 1)

            def turn_weights(g, k):
                pe.wait_ge(p_done, g + 1)
                for b in range(GB):
                    r = nc.tensor.transpose(bank(k)[0:3 * E, b * P:(b + 1) * P], p3f[:, b, :], ident[:, :])
                r.then_inc(pT3_ready, 1)

            def start_y(g):
                pe.wait_ge(split_done, g + 1)
                pe.wait_ge(z_relu, DC * (g + 1))
                pe.wait_ge(xd_done, g + 1)
                for c in range(DC):
                    for b in range(GB):
                        r = mm(bank(c)[:, b * P:(b + 1) * P], xD[:, b, c * P:(c + 1) * P], ident[:, :],
                               start=(b == 0), stop=False, skip_group_check=True)
                r.then_inc(y_init, 1)

            def group(i, ffn, more=True):
                f0 = (i - 1) * NE
                with pe.Fori(0, E // 2) as ee:
                    for h in range(2):
                        e = ee * 2 + h
                        for j in range(NJ):
                            n = e * NJ + j
                            nn = i * NS + n
                            half = h
                            if j == NJ - 1:
                                half = 1 - h
                                pe.wait_ge(stage_in, 48 * (9 * i + 2 + e))
                            pe.wait_ge(c_copied, nn + 1)
                            spread_b((j + 1) % 2, (j + 1) % NJ, half)
                            if ffn and j != 4:
                                ffn_piece(f0 + 1 + e, e + 1, j)
                            for c in range(DC):
                                if c == 2:
                                    pe.wait_ge(ub_done, 3 * nn + 3)
                                    spread_c((j + 1) % 2, (j + 1) % NJ, half)
                                    if ffn and j == 4:
                                        ffn_piece(f0 + 1 + e, e + 1, j)
                                pe.wait_ge(hc_done, 4 * nn + c + 6)
                                mm(bank(c), ident[:, :], hC[:, c, :], start=False, stop=False,
                                   skip_group_check=True).then_inc(y_added, 1)
                if ffn:
                    pe.wait_ge(acc_done, 4 * (f0 + NE) + 1)
                pe.wait_ge(y_copied, DC * (i + 1))
                for b in range(GB):
                    k_sum(bank(4 + b), lambda k: yT[:, k, b * P:(b + 1) * P],
                          lambda k: w_out[:, k, :]).then_inc(op_ready, 1)
                context(i)
                pe.wait_ge(x1_done, GB * (i + 1))
                turn(x1, (0, 1, 2, 3), x1T_ready)
                pe.wait_ge(x1T_done, DC * (i + 1))
                pe.wait_ge(k_done, i + 1)
                pe.wait_ge(v_done, i + 1)
                for c in range(DC):
                    k_sum(bank(4 + c), lambda k: w_q[:, k, c * P:(c + 1) * P],
                          lambda k: x1T[:, k, :]).then_inc(q_ready, 1)

                def scores(b):
                    bb = i * GB + b
                    if b == 0:
                        pe.wait_ge(k_spread, 16 * HEADS * (i + 1))
                        pe.wait_ge(q_done, DC * (i + 1))
                    else:
                        pe.wait_ge(s_added, HPG * bb)
                    for c in range(KV):
                        for j in range(HPG):
                            r = mm(bank(j)[:, c * P:(c + 1) * P], qT[j * DH:(j + 1) * DH, c, b * P:(b + 1) * P],
                                   kT[j * DH:(j + 1) * DH, c, b * P:(b + 1) * P], start=True, stop=True)
                    r.then_inc(s_ready, 1)

                def turn_ao(b):
                    pe.wait_ge(ao_normed, i * GB + b + 1)
                    for c in range(KV):
                        r = nc.tensor.transpose(bank(6)[:, c * P:(c + 1) * P], ao_q[:, c * P:(c + 1) * P], ident[:, :])
                    r.then_inc(aoT_ready, 1)

                def project_ao(b):
                    pe.wait_ge(aoT_done, i * GB + b + 1)
                    k_sum(bank(7), lambda k: aoT[:, k, b * P:(b + 1) * P], lambda k: w_o[:, k, :]).then_inc(wo_ready, 1)

                scores(0)
                for b in range(GB):
                    bb = i * GB + b
                    if b + 1 < GB:
                        scores(b + 1)
                    if b >= 1:
                        turn_ao(b - 1)
                    for c in range(KV):
                        pe.wait_ge(s_exp, HEADS * bb + HPG * (c + 1))
                        if c or b or ffn:
                            pe.wait_ge(pt_done, KV * bb + c)
                        for j in range(HPG):
                            r = nc.tensor.transpose(bank(4 + c % 2)[:, j * P:(j + 1) * P], probs[b % 2][:, j, c, :], ident[:, :])
                        r.then_inc(pt_ready, 1)
                    if b >= 1:
                        project_ao(b - 1)
                    for c in range(KV):
                        pe.wait_ge(pt_done, KV * bb + c + 2)
                        if c == 2:
                            pe.wait_ge(wo_used, bb + 1)
                        for j in range(HPG):
                            o = ((c % 2) * HPG + j) * (DH + 1)
                            r = mm(bank(6 + c // 2)[:, o:o + DH + 1], pT[:, c, j * P:(j + 1) * P], v_sb[:, b, c, :],
                                   start=True, stop=True)
                    r.then_inc(ao_ready, 1)
                pe.wait_ge(s_added, HPG * GB * (i + 1))
                if more:
                    turn_xhat(i + 1)
                turn_ao(GB - 1)
                project_ao(GB - 1)
                if more:
                    project_x(i + 1)
                    pe.wait_ge(split_done, i + 2)
                pe.wait_ge(x2_done, GB * (i + 1))
                turn(acc, (6, 7, 0, 1), x2T_ready)
                if more:
                    pe.wait_ge(z_relu, DC * (i + 2))
                for k in range(DC):
                    pe.wait_ge(x2T_done, DC * i + k + 1)
                    for h in range(2):
                        r = mm(bank(4)[0:2 * E, :], w_router[:, k, :, :].rearrange("p h e -> p (h e)"),
                               x2T[:, h, k, :], start=(k + h == 0), stop=(k + h == DC))
                r.then_inc(lgT_ready, 1)
                ffn_piece(i * NE, 0, 0)
                pe.wait_ge(lgT_done, i + 1)
                for b in range(GB):
                    r = mm(bank(5)[:, b * 2 * E:(b + 1) * 2 * E], lgT[:, b * P:(b + 1) * P],
                           ident[0:2 * E, 0:2 * E], start=True, stop=True)
                r.then_inc(lg_ready, 1)
                ffn_piece(i * NE, 0, 1)
                if more:
                    start_y(i + 1)
                ffn_piece(i * NE, 0, 2)
                ffn_piece(i * NE, 0, 3)
                if more:
                    pe.wait_ge(stage_in, 48 * (9 * i + 10))
                    spread_b(0, 0, 0)
                ffn_piece(i * NE, 0, 4)
                ffn_piece(i * NE, 0, 5)
                turn_weights(i, 5)
                ffn_piece(i * NE, 0, 6)
                pe.wait_ge(pT3_done, i + 1)
                if more:
                    spread_c(0, 0, 0)
                ffn_piece(i * NE, 0, 7)

            pe.wait_ge(first_in, 16 * FIRST_LOADS)
            turn_xhat(0)
            project_x(0)
            start_y(0)
            pe.wait_ge(stage_in, 48)
            spread_b(0, 0, 0)
            spread_c(0, 0, 0)
            pe.wait_ge(weights_in, 16 * WEIGHT_LOADS)
            group(0, False)
            with pe.Fori(1, GROUPS - 1) as i:
                group(i, True)
            group(GROUPS - 1, True, more=False)
            with pe.Fori(1, NE) as e:
                for j in range(8):
                    ffn_piece((GROUPS - 1) * NE + e, e, j)

        @block.scalar
        def _(act):
            act_fn = nc.scalar.activation

            def ffn_copy(f):
                act.wait_ge(pb_ready, f + 1)
                act.wait_ge(pg_done, 2 * f + 1)
                act_fn(pbc[:, :], bank(7), ACT.Copy).then_inc(pb_copied, 1)

            def ffn_tanh(f, c):
                act.wait_ge(pg_done, 2 * f + c + 2)
                act.wait_ge(hT_done, 2 * f + c + 1)
                act_fn(th[:, :], pG[:, :], ACT.Tanh, scale=0.5).then_inc(th_done, 1)

            def ffn_high(f, c):
                act.wait_ge(h_done, 2 * f + c + 1)
                act_fn(hT[:, 0, c, :], th[:, :], ACT.Copy).then_inc(hh_done, 1)

            def exps(i, n, c):
                nn = i * NS + n
                act.wait_ge(scan_done, 4 * nn + c + 2)
                act_fn(dA[:, c, :, 1:P], dtT[:, c, :].rearrange("p (b t) -> p b t", b=GB)[:, :, 1:P], ACT.Exp,
                       scale=a_neg[:, c, bass.ds(n, 1)]).then_inc(da_ready, 1)

            def context(g):
                for c in range(DC):
                    act.wait_ge(cT_ready, DC * g + c + 1)
                    act_fn(ctxT[:, c, :], bank(c), ACT.Copy).then_inc(cT_done, 1)
                act.wait_ge(k_ready, g + 1)
                act_fn(k_one[:, :], bank(4), ACT.Copy).then_inc(k_done, 1)

            def turned_xhat(g):
                for c in range(DC):
                    act.wait_ge(xhT_ready, DC * g + c + 1)
                    act_fn(xnT[:, c, :], bank(c), ACT.Identity, scale=chan[:, 0, c:c + 1],
                           bias=chan[:, 1, c:c + 1]).then_inc(xn_done, 1)

            def project_x(g):
                act.wait_ge(proj_ready, 2 * g + 2)
                act_fn(delta, bank(0), ACT.Copy).then_inc(delta_done, 1)
                for c, k in enumerate((2, 3, 4, 5)):
                    act.wait_ge(z_ready, DC * g + c + 1)
                    act_fn(dtT[:, c, :], bank(k), ACT.Abs, bias=chan[:, 2, c:c + 1]).then_inc(z_abs, 1)
                    act_fn(uT[:, c, :], bank(k), ACT.Relu, bias=chan[:, 2, c:c + 1]).then_inc(z_relu, 1)

            def softplus_exp(g):
                act.wait_ge(z_abs, DC * (g + 1))
                for c in range(DC):
                    act_fn(dtT[:, c, :], dtT[:, c, :], ACT.Exp, scale=-1.0).then_inc(act_link, 1)

            def softplus_log(g):
                act.wait_ge(act_link, DC * (g + 1))
                for c in range(DC):
                    act_fn(dtT[:, c, :], dtT[:, c, :], ACT.Ln, bias=1.0).then_inc(z_log, 1)

            def turned_weights(g, k):
                act.wait_ge(pT3_ready, g + 1)
                act_fn(p_T3[0:3 * E, :], bank(k)[0:3 * E, :], ACT.Copy).then_inc(pT3_done, 1)

            def group(i, ffn, more=True):
                f0 = (i - 1) * NE
                act.wait_ge(u_done, i + 1)
                with act.Fori(0, E // 2) as ee:
                    for h in range(2):
                        e = ee * 2 + h
                        f = f0 + 1 + e
                        for j in range(NJ):
                            n = e * NJ + j
                            nn = i * NS + n
                            act.wait_ge(b_ready, i * (NS + 1) + n + 1)
                            act.wait_ge(ub3_done, nn + 1)
                            act_fn(bc_sb[:, 0, j % 2, :], bank(4 + j % 2), ACT.Copy).then_inc(b_copied, 1)
                            exps(i, n, 0)
                            exps(i, n, 1)
                            act.wait_ge(c_ready, i * (NS + 1) + n + 1)
                            act.wait_ge(hc_done, 4 * nn + 1)
                            act_fn(bc_sb[:, 1, j % 2, :], bank(5 - j % 2), ACT.Copy).then_inc(c_copied, 1)
                            if ffn and j in (1, 3):
                                ffn_tanh(f, j // 2)
                            exps(i, n, 2)
                            exps(i, n, 3)
                            if ffn and j in (2, 4):
                                ffn_high(f, j // 2 - 1)
                            if ffn and j == 0:
                                ffn_copy(f)
                act.wait_ge(y_added, 4 * NS * (i + 1) + 4)
                for c in range(2):
                    act_fn(yT[:, c, :], bank(c), ACT.Copy).then_inc(y_copied, 1)
                context(i)
                for c in range(DC):
                    act.wait_ge(x1T_ready, DC * i + c + 1)
                    act_fn(x1T[:, c, :], bank(c), ACT.Copy).then_inc(x1T_done, 1)
                for c in range(DC):
                    act.wait_ge(q_ready, DC * i + c + 1)
                    act_fn(qT[:, c, :], bank(4 + c), ACT.Copy, scale=float(1.0 / np.sqrt(DH))).then_inc(q_done, 1)

                def softmax_exp(b):
                    act.wait_ge(s_max, i * GB + b + 1)
                    for c in range(KV):
                        for j in range(HPG):
                            r = j * KV + c
                            act_fn(probs[b % 2][:, j, c, :], probs[b % 2][:, j, c, :], ACT.Exp,
                                   bias=mx[:, b % 2, r:r + 1]).then_inc(s_exp, 1)

                def turned_probs(b):
                    bb = i * GB + b
                    for c in range(KV):
                        act.wait_ge(pt_ready, KV * bb + c + 1)
                        act.wait_ge(ao_ready, bb + 1)
                        act_fn(pT[:, c, :], bank(4 + c % 2), ACT.Copy).then_inc(pt_done, 1)

                def turned_ao(b):
                    act.wait_ge(aoT_ready, i * GB + b + 1)
                    act_fn(aoT[:, :, b * P:(b + 1) * P], bank(6).rearrange("p (c q) -> p c q", c=KV),
                           ACT.Copy).then_inc(aoT_done, 1)

                softmax_exp(0)
                turned_probs(0)
                for b in range(1, GB):
                    softmax_exp(b)
                    turned_ao(b - 1)
                    turned_probs(b)
                if more:
                    turned_xhat(i + 1)
                turned_ao(GB - 1)
                if more:
                    project_x(i + 1)
                for c, k in enumerate((6, 7, 0, 1)):
                    act.wait_ge(x2T_ready, DC * i + c + 1)
                    act_fn(x2T[:, 0, c, :], bank(k), ACT.Copy).then_inc(x2T_high, 1)
                if more:
                    softplus_exp(i + 1)
                ffn_copy(i * NE)
                if more:
                    softplus_log(i + 1)
                act.wait_ge(lg_done, i + 1)
                act_fn(el[:, :, :], lg[:, :, :], ACT.Exp, scale=-1.0).then_inc(lg_exp, 1)
                act.wait_ge(lg_ready, i + 1)
                for c in range(2):
                    ffn_tanh(i * NE, c)
                    ffn_high(i * NE, c)
                turned_weights(i, 5)

            act.wait_ge(first_in, 16 * FIRST_LOADS)
            act_fn(a_neg[:, :, :], a_neg[:, :, :], ACT.Exp).then_inc(a_exp, 1)
            act.wait_ge(hc_done, 5)
            turned_xhat(0)
            project_x(0)
            softplus_exp(0)
            softplus_log(0)
            group(0, False)
            with act.Fori(1, GROUPS - 1) as i:
                group(i, True)
            group(GROUPS - 1, True, more=False)

            with act.Fori(1, NE) as e:
                f = (GROUPS - 1) * NE + e
                ffn_copy(f)
                for c in range(2):
                    ffn_tanh(f, c)
                    ffn_high(f, c)

        @block.vector
        def _(dve):
            v = nc.vector

            class Link:

                def __init__(self, s, per):
                    self.sem, self.per, self.base, self.n = s, per, 0, 0

                def start(self, turn):
                    self.base, self.n = turn * self.per, 0

                def __call__(self, ins):
                    ins.then_inc(self.sem, 1)
                    self.n += 1
                    dve.wait_ge(self.sem, self.base + self.n)

                def end(self):
                    assert self.n == self.per, self.n

            link = Link(dve_link, 19)
            pre = Link(pre_link, 7)
            ln = Link(ln_link, 17)

            def norm(number, src, dst, done):
                ln.start(number)
                for b in range(GB):
                    last = v.bn_stats(stats[:, b, :], src[:, b, :])
                ln(last)
                v.memset(nt[:, :], 0.0)
                for b in range(GB):
                    last = v.bn_aggr(mv[:, b, :], stats[:, b, :])
                ln(last)
                ln(v.tensor_scalar(mv[:, :, 1], mv[:, :, 1], EPS, None, ALU.add))
                ln(v.tensor_scalar(rseed[:, :], mv[:, :, 1].bitcast(I32), 1, None, ALU.logical_shift_right))
                ln(v.tensor_scalar(rstd[:, :].bitcast(I32), rseed[:, :], -1, RSQRT_SEED, ALU.mult, ALU.add))
                for _ in range(4):
                    ln(v.tensor_tensor(nt[:, :], rstd[:, :], rstd[:, :], ALU.mult))
                    ln(v.scalar_tensor_tensor(nt[:, :], nt[:, :], -0.5, mv[:, :, 1], ALU.mult, ALU.mult))
                    ln(v.scalar_tensor_tensor(rstd[:, :], nt[:, :], 1.5, rstd[:, :], ALU.add, ALU.mult))
                ln.end()
                for b in range(GB):
                    v.tensor_scalar(dst[:, b, :], src[:, b, :], mv[:, b, 0:1], rstd[:, b:b + 1],
                                    ALU.subtract, ALU.mult).then_inc(done, 1)

            def ffn_pg(f, c):
                dve.wait_ge(g_ready, 2 * f + c + 1)
                dve.wait_ge(pb_copied, f + 1)
                v.tensor_tensor(pG[:, :], bank(6), pbc[:, :], ALU.mult).then_inc(pg_done, 1)

            def ffn_h(f, c):
                dve.wait_ge(th_done, 2 * f + c + 1)
                v.scalar_tensor_tensor(th[:, :], th[:, :], 1.0, pG[:, :], ALU.add, ALU.mult).then_inc(s_done, 1)
                dve.wait_ge(s_done, 2 * f + c + 1)
                dve.wait_ge(up_ready, 2 * f + c + 2)
                v.scalar_tensor_tensor(th[:, :], th[:, :], 0.5, bank(7), ALU.mult, ALU.mult).then_inc(h_done, 1)

            def ffn_low(f, c):
                dve.wait_ge(hh_done, 2 * f + c + 1)
                v.tensor_tensor(hT[:, 1, c, :], th[:, :], hT[:, 0, c, :].bitcast(F32),
                                ALU.subtract).then_inc(hT_done, 1)

            def ffn_acc(f, e, b):
                dve.wait_ge(d_ready, 4 * f + b + 2)
                v.scalar_tensor_tensor(acc[:, b, :], bank(6 + b % 2), p_t[:, b, bass.ds(e, 1)], acc[:, b, :],
                                       ALU.mult, ALU.add).then_inc(acc_done, 1)

            def ffn_piece(f, e, j):
                if j in (0, 2):
                    ffn_pg(f, j // 2)
                elif j in (1, 3):
                    ffn_h(f, j // 2)
                else:
                    ffn_acc(f, e, j - 4)

            def whole_expert(f, e):
                for j in range(8):
                    ffn_piece(f, e, j)
                    if j in (1, 3):
                        ffn_low(f, j // 2)

            def split_tile(f, q):
                dst = w_gu[:, :, q, :] if q < DC else w_down[:, :, q - DC, :]
                src = split_in[q % 2][:, :]
                dve.wait_ge(wsplit_in[q % 2], 32 * (3 * f + q // 2 + 1))
                if q in (0, DC) and not (isinstance(f, int) and f == 0):
                    dve.wait_ge(down_out if q else gu_out, 16 * f)
                v.tensor_copy(dst[:, 0, :], src).then_inc(wsplit_high, 1)
                dve.wait_ge(wsplit_high, 6 * f + q + 1)
                v.tensor_tensor(dst[:, 1, :], src, dst[:, 0, :].bitcast(F32), ALU.subtract).then_inc(wsplit_done, 1)

            def values(g):
                dve.wait_ge(v_ready, g + 1)
                v.tensor_copy(v_sb[:, :, :, 0:DH], bank(5).rearrange("p (b c d) -> p b c d", b=GB, c=KV)).then_inc(v_done, 1)

            def normed_x(number, g):
                dve.wait_ge(x_in, 16 * (g + 1))
                norm(number, x_raw, xhat, xhat_done)

            def split_bc(g):
                dve.wait_ge(proj_ready, 2 * g + 1)
                v.memset(dA[:, :, :, 0:1], 0.0)
                pre.start(g)
                pre(v.tensor_copy(bc_parts[:, 0, :], bank(1)))
                pre(v.tensor_tensor(resid, bank(1), bc_parts[:, 0, :], ALU.subtract))
                pre(v.tensor_copy(bc_parts[:, 1, :], resid))
                v.tensor_tensor(bc_parts[:, 2, :], resid, bc_parts[:, 1, :], ALU.subtract).then_inc(split_done, 1)

            def dt_and_u(g, tiles):
                for c in tiles:
                    dve.wait_ge(z_log, DC * g + c + 1)
                    dve.wait_ge(z_relu, DC * g + c + 1)
                    pre(v.tensor_tensor(dtT[:, c, :], dtT[:, c, :], uT[:, c, :], ALU.add))
                    last = v.tensor_tensor(uT[:, c, :], dtT[:, c, :], xnT[:, c, :], ALU.mult)
                if c == DC - 1:
                    last.then_inc(u_done, 1)
                    pre.end()

            def group(i, ffn, more=True):
                f0 = (i - 1) * NE
                n0 = 4 * i if ffn else 1
                link.start(i)
                dve.wait_ge(u_done, i + 1)
                v.memset(nt[:, :], 0.0)
                with dve.Fori(0, E // 2) as ee:
                    for h in range(2):
                        e = ee * 2 + h
                        for j in range(NJ):
                            nn = i * NS + e * NJ + j
                            dve.wait_ge(b_copied, nn + 1)
                            for c in range(3):
                                dve.wait_ge(scan_done, 4 * nn + c + 2)
                                v.tensor_tensor(uB[:, c, :], uT[:, c, :], bank(4 + j % 2), ALU.mult).then_inc(ub_done, 1)
                            for c in range(DC):
                                if c == 3:
                                    dve.wait_ge(ub3_done, nn + 3)
                                else:
                                    dve.wait_ge(ub_done, 3 * nn + c + 1)
                                dve.wait_ge(da_ready, 4 * nn + c + 1)
                                dve.wait_ge(hc_done, 4 * nn + c + 2)
                                v.tensor_tensor_scan(hs[:, c, :], dA[:, c, :, :].rearrange("p b t -> p (b t)"),
                                                     uB[:, c, :] if c < 3 else ub3(j % 2),
                                                     0.0, ALU.mult, ALU.add).then_inc(scan_done, 1)
                                if ffn and j in (2, 4) and c == 1:
                                    ffn_low(f0 + 1 + e, j // 2 - 1)
                                if ffn and j == 5 and c == 1:
                                    ffn_piece(f0 + 1 + e, e, 4)
                            if ffn and j != 4:
                                ffn_piece(f0 + 1 + e, e, j)
                            elif not ffn and j < 6:
                                split_tile(1 + e, j)
                v.memset(nt[:, :], 0.0)
                dve.wait_ge(y_added, 4 * NS * (i + 1) + 4)
                for c in (2, 3):
                    v.tensor_copy(yT[:, c, :], bank(c)).then_inc(y_copied, 1)
                dve.wait_ge(mask_in, 16 * (i + 1))
                v.tensor_scalar(negm[:, :, :], masks[:, :, :], -NEG, NEG, ALU.mult, ALU.add).then_inc(negm_done, 1)
                for b in range(GB):
                    dve.wait_ge(op_ready, GB * i + b + 1)
                    v.tensor_tensor(x1[:, b, :], bank(4 + b), x_raw[:, b, :], ALU.add).then_inc(x_used, 1)
                dve.wait_ge(x_used, GB * (i + 1))
                norm(n0, x1, x1, x1_done)
                values(i)
                if ffn:
                    norm(n0 + 1, acc, acc, out_done)
                    n0 = n0 + 1

                def shift(b):
                    bb = i * GB + b
                    p4 = probs[b % 2]
                    dve.wait_ge(s_ready, bb + 1)
                    dve.wait_ge(bias_done, bb + 1)
                    if b >= 2:
                        dve.wait_ge(pt_ready, KV * (bb - 1))
                    for j in range(HPG):
                        v.tensor_tensor(p4[:, j, :, :], bank(j).rearrange("p (c k) -> p c k", c=KV),
                                        bias[:, j, :, :], ALU.add).then_inc(s_added, 1)
                    dve.wait_ge(s_added, HPG * (bb + 1))
                    link(v.tensor_reduce(rs[:, :], p4.rearrange("p j c k -> p (j c) k"), AX.X, ALU.max))
                    v.tensor_scalar(mx[:, b % 2, :], rs[:, :], -1.0, None, ALU.mult).then_inc(s_max, 1)

                def normed_ao(b):
                    dve.wait_ge(ao_ready, i * GB + b + 2)
                    o = ps[:, 6:8, 0:2 * HPG * (DH + 1)].rearrange("p a (h d) -> p a h d", d=DH + 1)
                    r = sums[:, :].rearrange("p (a h) -> p a h", a=2)
                    link(v.reciprocal(r, o[:, :, :, DH]))
                    v.tensor_tensor(ao_q[:, :].rearrange("p (a h d) -> p a h d", a=2, d=DH), o[:, :, :, 0:DH],
                                    r.unsqueeze(3).to_broadcast([P, 2, 2 * HPG, DH]), ALU.mult).then_inc(ao_normed, 1)

                def residual(b):
                    dve.wait_ge(wo_ready, i * GB + b + 1)
                    if ffn:
                        dve.wait_ge(stored, 16 * i)
                    v.tensor_tensor(acc[:, b, :], bank(7), x1[:, b, :], ALU.add).then_inc(wo_used, 1)

                shift(0)
                shift(1)
                if more:
                    dve.wait_ge(cT_ready, DC * (i + 1))
                    n0 = n0 + 1
                    normed_x(n0, i + 1)
                normed_ao(0)
                for b in range(1, GB):
                    if b + 1 < GB:
                        shift(b + 1)
                    residual(b - 1)
                    normed_ao(b)
                residual(GB - 1)
                dve.wait_ge(wo_used, GB * (i + 1) + 1)
                norm(n0 + 1, acc, acc, x2_done)
                if more:
                    split_bc(i + 1)
                for c, k in enumerate((6, 7, 0, 1)):
                    dve.wait_ge(x2T_high, DC * i + c + 1)
                    v.tensor_tensor(x2T[:, 1, c, :], bank(k), x2T[:, 0, c, :].bitcast(F32),
                                    ALU.subtract).then_inc(x2T_done, 1)
                dve.wait_ge(lgT_ready, i + 1)
                v.tensor_copy(lgT, bank(4)[0:2 * E, :]).then_inc(lgT_done, 1)
                f = i * NE
                ffn_pg(f, 0)
                dve.wait_ge(lg_ready, i + 1)
                v.tensor_reduce(lg[:, :, :], bank(5)[:, 0:GB * 2 * E].rearrange("p (b h e) -> p b e h", b=GB, h=2),
                                AX.X, ALU.add).then_inc(lg_done, 1)
                dve.wait_ge(lg_done, i + 1)
                other = lg[:, :, :].unsqueeze(2).to_broadcast([P, GB, E, E])
                own = lg[:, :, :].unsqueeze(3).to_broadcast([P, GB, E, E])
                v.tensor_tensor(gt[:, :, :, :], other, own, ALU.is_gt)
                link(v.tensor_tensor(eq[:, :, :, :], other, own, ALU.is_equal))
                link(v.tensor_tensor(eq[:, :, :, :], eq[:, :, :, :],
                                     tri[:, :, :].unsqueeze(1).to_broadcast([P, GB, E, E]), ALU.mult))
                link(v.tensor_tensor(gt[:, :, :, :], gt[:, :, :, :], eq[:, :, :, :], ALU.add))
                link(v.tensor_reduce(rank[:, :, :].rearrange("p b e -> p (b e)"),
                                     gt[:, :, :, :].rearrange("p b e o -> p (b e) o"), AX.X, ALU.add))
                ffn_h(f, 0)
                ffn_low(f, 0)
                if more:
                    dt_and_u(i + 1, (0, 1))
                ffn_pg(f, 1)
                dve.wait_ge(lg_exp, i + 1)
                link(v.tensor_scalar(el[:, :, :], el[:, :, :], 1.0, None, ALU.add))
                link(v.reciprocal(el[:, :, :], el[:, :, :]))
                link(v.scalar_tensor_tensor(p_t[:, :, 0:E], rank[:, :, :], 2.0, el[:, :, :], ALU.is_lt, ALU.mult))
                link(v.tensor_copy(p3b[:, :, 0:E], p_t[:, :, 0:E]))
                link(v.tensor_tensor(el[:, :, :], p_t[:, :, 0:E], p3b[:, :, 0:E], ALU.subtract))
                link(v.tensor_copy(p3b[:, :, E:2 * E], el[:, :, :]))
                link(v.tensor_tensor(p3b[:, :, 2 * E:], el[:, :, :], p3b[:, :, E:2 * E], ALU.subtract))
                v.tensor_copy(p3f[:, :, :], p3b[:, :, :]).then_inc(p_done, 1)
                link.end()
                ffn_h(f, 1)
                ffn_low(f, 1)
                if more:
                    dt_and_u(i + 1, (2, 3))
                for b in range(GB):
                    ffn_acc(f, E, b)

            for k, free in enumerate((up_ready, d_ready, acc_done, pg_done, hT_done, ao_ready, wo_used, pt_done,
                                      wsplit_done)):
                v.memset(mx[:, 0, k:k + 1], 0.0).then_inc(free, 1)
            v.memset(mx[:, 0, 15:16], 0.0).then_inc(scan_done, 5)
            v.memset(p_t[:, :, :], 1.0)
            v.memset(v_sb[:, :, :, :], 1.0)
            v.memset(p_T3[:, :], 1.0)
            normed_x(0, 0)
            split_tile(0, 0)
            split_tile(0, 1)
            dve.wait_ge(first_in, 16 * FIRST_LOADS)
            v.tensor_copy(pick_bc[:, :], pickb32[:, :])
            v.tensor_copy(pick_p[:, :], pickp32[:, :])
            dve.wait_ge(a_exp, 1)
            v.tensor_scalar(a_neg[:, :, :], a_neg[:, :, :], -1.0, None, ALU.mult)
            dve.wait_ge(y_added, 4)
            dve.wait_ge(hc_done, 5)
            split_bc(0)
            split_tile(0, 2)
            split_tile(0, 3)
            dt_and_u(0, range(DC))
            dve.wait_ge(weights_in, 16 * WEIGHT_LOADS)
            v.tensor_copy(w_router[:, :, 0, :], router32[:, :, :]).then_inc(router_split, 1)
            split_tile(0, 4)
            dve.wait_ge(router_split, 1)
            v.tensor_tensor(w_router[:, :, 1, :], router32[:, :, :], w_router[:, :, 0, :].bitcast(F32), ALU.subtract)
            split_tile(0, 5)
            group(0, False)
            with dve.Fori(1, GROUPS - 1) as i:
                group(i, True)
            group(GROUPS - 1, True, more=False)
            with dve.Fori(1, NE) as e:
                whole_expert((GROUPS - 1) * NE + e, e - 1)
            dve.wait_ge(acc_done, 4 * NE * GROUPS + 1)
            norm(4 * GROUPS - 1, acc, acc, out_done)

        @block.gpsimd
        def _(pool):
            g = nc.gpsimd

            def times_d(n):
                pool.wait_ge(x_in, 16 * (n + 1))
                g.tensor_tensor(xD[:, :, :], x_raw[:, :, :], d_row[:, :].unsqueeze(1).to_broadcast([P, GB, D]),
                                ALU.mult).then_inc(xd_done, 1)

            def group(i, ffn, more=True):
                with pool.Fori(0, E // 2) as ee:
                    for h in range(2):
                        for j in range(NJ):
                            nn = i * NS + (ee * 2 + h) * NJ + j
                            if h == 0 and j == 0:
                                pool.wait_ge(u_done, i + 1)
                                pool.wait_ge(y_init, i + 1)
                            pool.wait_ge(b_copied, nn + 1)
                            pool.wait_ge(scan_done, 4 * nn + 1)
                            g.tensor_tensor(ub3(j % 2), uT[:, 3, :], bc_sb[:, 0, j % 2, :], ALU.mult).then_inc(ub3_done, 1)
                            pool.wait_ge(c_copied, nn + 1)
                            for c in range(DC):
                                pool.wait_ge(scan_done, 4 * nn + c + 6)
                                pool.wait_ge(y_added, 4 * nn + c + 1)
                                g.tensor_tensor(hC[:, c, :], hs[:, c, :], bc_sb[:, 1, j % 2, :],
                                                ALU.mult).then_inc(hc_done, 1)

                def add_bias(b):
                    g.tensor_tensor(bias, alibi[:, :, :, :],
                                    negm[:, b, :].unsqueeze(1).unsqueeze(1).to_broadcast([P, HPG, KV, P]),
                                    ALU.add).then_inc(bias_done, 1)

                pool.wait_ge(negm_done, i + 1)
                add_bias(0)
                if ffn:
                    pool.wait_ge(out_done, GB * i)
                    pool.dma_start(out_g[i - 1], acc[:, :, :]).then_inc(stored, 16)
                for b in range(1, GB):
                    pool.wait_ge(s_added, HPG * (i * GB + b))
                    add_bias(b)
                if more:
                    pool.wait_ge(pt_ready, KV * GB * (i + 1))
                    times_d(i + 1)

            g.memset(bc_sb[:, :, :, :], 0.0).then_inc(y_added, 4)
            g.memset(hs[:, :, :], 0.0).then_inc(hc_done, 5)
            g.memset(uB3b[:, :], 0.0).then_inc(ub3_done, 2)
            pool.wait_ge(first_in, 16 * FIRST_LOADS)
            times_d(0)
            pool.wait_ge(weights_in, 16 * WEIGHT_LOADS)
            g.memset(mx[:, 1, 0:1], 0.0)
            group(0, False)
            with pool.Fori(1, GROUPS - 1) as i:
                group(i, True)
            group(GROUPS - 1, True, more=False)
            pool.wait_ge(out_done, GB * GROUPS)
            pool.dma_start(out_g[GROUPS - 1], acc[:, :, :]).then_inc(stored, 16)
            pool.wait_ge(stored, 16 * GROUPS)

def kernel(**inputs):
    import concourse.bacc as bacc
    from concourse.bass_utils import run_bass_kernel_spmd

    def arr(name):
        return np.asarray(inputs[name])

    picks = np.tile(np.eye(NJ, dtype=np.float32), (3, 1))
    pickp = np.zeros((25, NE), np.float32)
    pickp[24, 0] = 1
    for e in range(E):
        pickp[[e, E + e, 2 * E + e], 1 + e] = 1
    m0 = np.float32(2.0 ** (-8.0 / HEADS))
    slopes = (m0 ** np.arange(1, HEADS + 1, dtype=np.float32)).reshape(KV, HPG).T
    rel = np.arange(P, dtype=np.float32)[None, :] - np.arange(P, dtype=np.float32)[:, None]
    alibi = slopes[None, :, :, None] * rel[:, None, None, :]
    tri = np.broadcast_to(np.tril(np.ones((E, E), np.float32), -1), (P, E, E))
    arrays = {
        "x": arr("x"), "ctx": arr("ctx_2048"), "mask": arr("mask_BxS2_bf1").view(np.uint8),
        "chan": np.stack([arr("L0_attn_norm_w"), arr("L0_attn_norm_b"), arr("L0_attn_dt_proj_b")])
                .reshape(3, DC, P).transpose(2, 0, 1),
        "D": arr("L0_attn_D_param"),
        "xprojT": arr("L0_attn_x_proj_w").T, "dtprojT": arr("L0_attn_dt_proj_w").T,
        "A_log": arr("L0_attn_A_log"), "outT": arr("L0_attn_out_proj_w").T,
        "Wq": arr("L0_xattn_Wq"), "Wk": arr("L0_xattn_Wk"), "Wv": arr("L0_xattn_Wv"), "Wo": arr("L0_xattn_Wo"),
        "router": arr("L0_ffn_router_w"), "gate_up": arr("L0_ffn_gate_up_w"), "down": arr("L0_ffn_down_w"),
        "sgate": arr("L0_ffn_shared_gate_w"), "sup": arr("L0_ffn_shared_up_w"), "sdown": arr("L0_ffn_shared_down_w"),
        "ident": np.eye(P, dtype=np.float32), "picks": picks, "pickp": pickp,
        "alibi": alibi.astype(np.float32), "tri": tri,
    }
    nc = bacc.Bacc("TRN2", target_bir_lowering=False, num_devices=1)
    feed, aps = {}, {}
    for name, v in arrays.items():
        v = np.ascontiguousarray(v)
        feed[f"in_{name}"] = v
        aps[name] = nc.dram_tensor(f"in_{name}", v.shape, mybir.dt.from_np(v.dtype), kind="ExternalInput").ap()
    out = nc.dram_tensor("out", (B, P, D), F32, kind="ExternalOutput").ap()
    decoder_layer_kernel(nc, aps, out)
    r = run_bass_kernel_spmd(nc, [feed], core_ids=[0])
    return r.results[0]["out"]
```
